# Optimizing a Trainium2 kernel written in Bass

```python
import numpy as np
import jax
import jax.numpy as jnp

def _softmax(x, axis=-1):
    return jax.nn.softmax(x, axis=axis)

def _gelu(x):
    return jax.nn.gelu(x, approximate=True)

def _silu(x):
    return jax.nn.silu(x)

def _sigmoid(x):
    return jax.nn.sigmoid(x)

def _layernorm(x, axis=-1, eps=1e-05):
    m = jnp.mean(x, axis=axis, keepdims=True)
    v = jnp.var(x, axis=axis, keepdims=True)
    return (x - m) / jnp.sqrt(v + eps)

def _scatter_add(tgt, idx, src, axis=0):
    return tgt.at[idx].add(src)

def _segment_sum(src, seg, n):
    return jax.ops.segment_sum(src, seg, n)
kernel_name = 'mk_xattn_seq_d2_seqx_r8_6352cd'

def setup_inputs(seed: int=0):
    np.random.seed(seed)
    _w = jnp.asarray

    def _rec_inputs():
        import jax
        import jax.numpy as jnp
        _rk = jax.random.key(seed)
        x = -0.0001548 + 1 * jax.random.normal(jax.random.fold_in(_rk, 1), (64, 128, 160), jnp.float32)
        _lenS = 128 - jax.random.randint(jax.random.fold_in(_rk, 7), (64,), 0, max(1, 128 // 4) + 1, jnp.int32)
        _lenS2 = 77 - jax.random.randint(jax.random.fold_in(_rk, 8), (64,), 0, max(1, 77 // 4) + 1, jnp.int32)
        _ctx_2048P = jax.random.normal(jax.random.fold_in(_rk, 11), (64, 16, 256), jnp.float32)
        _ctx_2048c = jax.random.dirichlet(jax.random.fold_in(_rk, 511), 0.3 * jnp.ones((16,), jnp.float32), (64, 77))
        _ctx_2048t = jnp.einsum('bsk,bkd->bsd', _ctx_2048c, _ctx_2048P)
        _ctx_2048t = _ctx_2048t * jax.lax.rsqrt(jnp.mean(jnp.square(_ctx_2048t)) + 1e-12) * 0.953939
        ctx_2048 = 0.00208318 + 0.999174 * (_ctx_2048t + 0.3 * jax.random.normal(jax.random.fold_in(_rk, 611), (64, 77, 256), jnp.float32))
        fside_S_0 = jax.random.uniform(jax.random.fold_in(_rk, 12), (128,), jnp.float32, 0.0, 0.999706)
        return (x, ctx_2048, fside_S_0)
    x, ctx_2048, fside_S_0 = _rec_inputs()

    def _L0_xattn_setup():
        import jax, jax.numpy as jnp
        import numpy as np
        DIM = 160
        HEADS = 20
        DHEAD = 64
        CTX_DIM = 256
        INNER = HEADS * DHEAD
        FF_INNER = 4 * DIM
        SCALE = DHEAD ** (-0.5)
        EPS = 1e-05

        def _layer_norm(x, g, b):
            m = jnp.mean(x, axis=-1, keepdims=True)
            v = jnp.mean(jnp.square(x - m), axis=-1, keepdims=True)
            return (x - m) * jax.lax.rsqrt(v + EPS) * g + b

        def _attention(x, ctx, wq, wk, wv, wo, bo):
            B, N, _ = x.shape
            M = ctx.shape[1]
            q = (x @ wq).reshape(B, N, HEADS, DHEAD).transpose(0, 2, 1, 3)
            k = (ctx @ wk).reshape(B, M, HEADS, DHEAD).transpose(0, 2, 1, 3)
            v = (ctx @ wv).reshape(B, M, HEADS, DHEAD).transpose(0, 2, 1, 3)
            sim = jnp.einsum('bhid,bhjd->bhij', q, k) * SCALE
            attn = jax.nn.softmax(sim, axis=-1)
            out = jnp.einsum('bhij,bhjd->bhid', attn, v)
            out = out.transpose(0, 2, 1, 3).reshape(B, N, INNER)
            return out @ wo + bo

        def _geglu_ff(x, w1, b1, w2, b2):
            h = x @ w1 + b1
            a, gate = jnp.split(h, 2, axis=-1)
            return a * jax.nn.gelu(gate, approximate=False) @ w2 + b2
        key = jax.random.key(seed)
        ks = jax.random.split(key, 16)
        s = 0.02
        d = {'x': jax.random.normal(ks[0], (2, 256, DIM), jnp.float32), 'context': jax.random.normal(ks[1], (2, 77, CTX_DIM), jnp.float32), 'a1_wq': jax.random.normal(ks[2], (DIM, INNER), jnp.float32) * s, 'a1_wk': jax.random.normal(ks[3], (DIM, INNER), jnp.float32) * s, 'a1_wv': jax.random.normal(ks[4], (DIM, INNER), jnp.float32) * s, 'a1_wo': jax.random.normal(ks[5], (INNER, DIM), jnp.float32) * s, 'a1_bo': jnp.zeros((DIM,), jnp.float32), 'a2_wq': jax.random.normal(ks[6], (DIM, INNER), jnp.float32) * s, 'a2_wk': jax.random.normal(ks[7], (CTX_DIM, INNER), jnp.float32) * s, 'a2_wv': jax.random.normal(ks[8], (CTX_DIM, INNER), jnp.float32) * s, 'a2_wo': jax.random.normal(ks[9], (INNER, DIM), jnp.float32) * s, 'a2_bo': jnp.zeros((DIM,), jnp.float32), 'ff_w1': jax.random.normal(ks[10], (DIM, 2 * FF_INNER), jnp.float32) * s, 'ff_b1': jnp.zeros((2 * FF_INNER,), jnp.float32), 'ff_w2': jax.random.normal(ks[11], (FF_INNER, DIM), jnp.float32) * s, 'ff_b2': jnp.zeros((DIM,), jnp.float32), 'ln1_g': jnp.ones((DIM,), jnp.float32), 'ln1_b': jnp.zeros((DIM,), jnp.float32), 'ln2_g': jnp.ones((DIM,), jnp.float32), 'ln2_b': jnp.zeros((DIM,), jnp.float32), 'ln3_g': jnp.ones((DIM,), jnp.float32), 'ln3_b': jnp.zeros((DIM,), jnp.float32)}
        return d
    _L0_xattn_all = _L0_xattn_setup()
    _L0_xattn_in = {k: v for k, v in _L0_xattn_all.items() if k in ('a1_wq', 'a1_wk', 'a1_wv', 'a1_wo', 'a1_bo', 'a2_wq', 'a2_wk', 'a2_wv', 'a2_wo', 'a2_bo', 'ff_w1', 'ff_b1', 'ff_w2', 'ff_b2', 'ln1_g', 'ln1_b', 'ln2_g', 'ln2_b', 'ln3_g', 'ln3_b')}
    del _L0_xattn_all

    def _L1_xattn_setup():
        import jax, jax.numpy as jnp
        import numpy as np
        HEADS = 20
        NUM_TOKENS = 4
        IP_SCALE = 1.0
        SEM_SCALE = 0.5
        RESCALE = 1.0
        EPS = 1e-12

        def _l2norm(x, axis=-1):
            n = jnp.sqrt(jnp.sum(x * x, axis=axis, keepdims=True))
            return x / jnp.maximum(n, EPS)
        key = jax.random.key(seed)
        ks = jax.random.split(key, 10)
        B, S, C = (2, 128, 160)
        T, E = (81, 256)
        inp = {'hidden_states': jax.random.normal(ks[0], (B, S, C), jnp.float32), 'encoder_hidden_states': jax.random.normal(ks[1], (B, T, E), jnp.float32), 'spatial_mask': jax.random.uniform(ks[2], (S,), jnp.float32), 'W_q': jax.random.normal(ks[3], (C, C), jnp.float32) * C ** (-0.5), 'W_k': jax.random.normal(ks[4], (E, C), jnp.float32) * E ** (-0.5), 'W_v': jax.random.normal(ks[5], (E, C), jnp.float32) * E ** (-0.5), 'W_k_ip': jax.random.normal(ks[6], (E, C), jnp.float32) * E ** (-0.5), 'W_v_ip': jax.random.normal(ks[7], (E, C), jnp.float32) * E ** (-0.5), 'W_out': jax.random.normal(ks[8], (C, C), jnp.float32) * C ** (-0.5), 'b_out': jnp.zeros((C,), jnp.float32)}
        return inp
    _L1_xattn_all = _L1_xattn_setup()
    _L1_xattn_in = {k: v for k, v in _L1_xattn_all.items() if k in ('W_q', 'W_k', 'W_v', 'W_k_ip', 'W_v_ip', 'W_out', 'b_out')}
    del _L1_xattn_all
    return {'x': x, 'ctx_2048': ctx_2048, 'fside_S_0': fside_S_0, 'L0_xattn_a1_wq': _L0_xattn_in['a1_wq'], 'L0_xattn_a1_wk': _L0_xattn_in['a1_wk'], 'L0_xattn_a1_wv': _L0_xattn_in['a1_wv'], 'L0_xattn_a1_wo': _L0_xattn_in['a1_wo'], 'L0_xattn_a1_bo': _L0_xattn_in['a1_bo'], 'L0_xattn_a2_wq': _L0_xattn_in['a2_wq'], 'L0_xattn_a2_wk': _L0_xattn_in['a2_wk'], 'L0_xattn_a2_wv': _L0_xattn_in['a2_wv'], 'L0_xattn_a2_wo': _L0_xattn_in['a2_wo'], 'L0_xattn_a2_bo': _L0_xattn_in['a2_bo'], 'L0_xattn_ff_w1': _L0_xattn_in['ff_w1'], 'L0_xattn_ff_b1': _L0_xattn_in['ff_b1'], 'L0_xattn_ff_w2': _L0_xattn_in['ff_w2'], 'L0_xattn_ff_b2': _L0_xattn_in['ff_b2'], 'L0_xattn_ln1_g': _L0_xattn_in['ln1_g'], 'L0_xattn_ln1_b': _L0_xattn_in['ln1_b'], 'L0_xattn_ln2_g': _L0_xattn_in['ln2_g'], 'L0_xattn_ln2_b': _L0_xattn_in['ln2_b'], 'L0_xattn_ln3_g': _L0_xattn_in['ln3_g'], 'L0_xattn_ln3_b': _L0_xattn_in['ln3_b'], 'L1_xattn_W_q': _L1_xattn_in['W_q'], 'L1_xattn_W_k': _L1_xattn_in['W_k'], 'L1_xattn_W_v': _L1_xattn_in['W_v'], 'L1_xattn_W_k_ip': _L1_xattn_in['W_k_ip'], 'L1_xattn_W_v_ip': _L1_xattn_in['W_v_ip'], 'L1_xattn_W_out': _L1_xattn_in['W_out'], 'L1_xattn_b_out': _L1_xattn_in['b_out']}

def reference(x, ctx_2048, fside_S_0, L0_xattn_a1_wq, L0_xattn_a1_wk, L0_xattn_a1_wv, L0_xattn_a1_wo, L0_xattn_a1_bo, L0_xattn_a2_wq, L0_xattn_a2_wk, L0_xattn_a2_wv, L0_xattn_a2_wo, L0_xattn_a2_bo, L0_xattn_ff_w1, L0_xattn_ff_b1, L0_xattn_ff_w2, L0_xattn_ff_b2, L0_xattn_ln1_g, L0_xattn_ln1_b, L0_xattn_ln2_g, L0_xattn_ln2_b, L0_xattn_ln3_g, L0_xattn_ln3_b, L1_xattn_W_q, L1_xattn_W_k, L1_xattn_W_v, L1_xattn_W_k_ip, L1_xattn_W_v_ip, L1_xattn_W_out, L1_xattn_b_out):
    import jax
    import jax.numpy as jnp

    def _L0_xattn_ref(x, context, a1_wq, a1_wk, a1_wv, a1_wo, a1_bo, a2_wq, a2_wk, a2_wv, a2_wo, a2_bo, ff_w1, ff_b1, ff_w2, ff_b2, ln1_g, ln1_b, ln2_g, ln2_b, ln3_g, ln3_b):
        import jax, jax.numpy as jnp
        import numpy as np
        DIM = 160
        HEADS = 20
        DHEAD = 64
        CTX_DIM = 256
        INNER = HEADS * DHEAD
        FF_INNER = 4 * DIM
        SCALE = DHEAD ** (-0.5)
        EPS = 1e-05

        def _layer_norm(x, g, b):
            m = jnp.mean(x, axis=-1, keepdims=True)
            v = jnp.mean(jnp.square(x - m), axis=-1, keepdims=True)
            return (x - m) * jax.lax.rsqrt(v + EPS) * g + b

        def _attention(x, ctx, wq, wk, wv, wo, bo):
            B, N, _ = x.shape
            M = ctx.shape[1]
            q = (x @ wq).reshape(B, N, HEADS, DHEAD).transpose(0, 2, 1, 3)
            k = (ctx @ wk).reshape(B, M, HEADS, DHEAD).transpose(0, 2, 1, 3)
            v = (ctx @ wv).reshape(B, M, HEADS, DHEAD).transpose(0, 2, 1, 3)
            sim = jnp.einsum('bhid,bhjd->bhij', q, k) * SCALE
            attn = jax.nn.softmax(sim, axis=-1)
            out = jnp.einsum('bhij,bhjd->bhid', attn, v)
            out = out.transpose(0, 2, 1, 3).reshape(B, N, INNER)
            return out @ wo + bo

        def _geglu_ff(x, w1, b1, w2, b2):
            h = x @ w1 + b1
            a, gate = jnp.split(h, 2, axis=-1)
            return a * jax.nn.gelu(gate, approximate=False) @ w2 + b2
        n = _layer_norm(x, ln1_g, ln1_b)
        x = x + _attention(n, n, a1_wq, a1_wk, a1_wv, a1_wo, a1_bo)
        n = _layer_norm(x, ln2_g, ln2_b)
        x = x + _attention(n, context, a2_wq, a2_wk, a2_wv, a2_wo, a2_bo)
        x = _geglu_ff(_layer_norm(x, ln3_g, ln3_b), ff_w1, ff_b1, ff_w2, ff_b2) + x
        return x

    def _L1_xattn_ref(hidden_states, encoder_hidden_states, spatial_mask, W_q, W_k, W_v, W_k_ip, W_v_ip, W_out, b_out):
        import jax, jax.numpy as jnp
        import numpy as np
        HEADS = 20
        NUM_TOKENS = 4
        IP_SCALE = 1.0
        SEM_SCALE = 0.5
        RESCALE = 1.0
        EPS = 1e-12

        def _l2norm(x, axis=-1):
            n = jnp.sqrt(jnp.sum(x * x, axis=axis, keepdims=True))
            return x / jnp.maximum(n, EPS)
        B, S, C = hidden_states.shape
        H = HEADS
        Dh = C // H
        attn_scale = Dh ** (-0.5)
        residual = hidden_states
        text_ehs = encoder_hidden_states[:, :-NUM_TOKENS]
        ip_ehs = encoder_hidden_states[:, -NUM_TOKENS:]

        def heads(x):
            return x.reshape(B, -1, H, Dh).transpose(0, 2, 1, 3)
        q = heads(hidden_states @ W_q)
        k_t = heads(text_ehs @ W_k)
        v_t = heads(text_ehs @ W_v)
        scores_t = jnp.einsum('bhsd,bhtd->bhst', q, k_t) * attn_scale
        probs_t = jax.nn.softmax(scores_t, axis=-1)
        text_out = jnp.einsum('bhst,bhtd->bhsd', probs_t, v_t)
        text_out = text_out.transpose(0, 2, 1, 3).reshape(B, S, C)
        k_ip = heads(ip_ehs @ W_k_ip)
        v_ip = heads(ip_ehs @ W_v_ip)
        attn_scores = jnp.einsum('bhsd,bhnd->bhsn', q, k_ip) * attn_scale
        qsem = jnp.einsum('bhst,bte->bhse', probs_t, text_ehs)
        qsem = _l2norm(qsem)
        ip_n = _l2norm(ip_ehs)
        sem = jnp.einsum('bhse,bne->bhsn', qsem, ip_n)
        sem = jax.lax.stop_gradient(sem)
        fused = attn_scores + SEM_SCALE * sem
        probs_ip = jax.nn.softmax(fused, axis=-1)
        probs_ip = probs_ip * spatial_mask[None, None, :, None]
        ip_out = jnp.einsum('bhsn,bhnd->bhsd', probs_ip, v_ip)
        ip_out = ip_out.transpose(0, 2, 1, 3).reshape(B, S, C)
        out = text_out + IP_SCALE * ip_out
        out = out @ W_out + b_out
        out = out + residual
        return out / RESCALE
    x = _L0_xattn_ref(x, ctx_2048, L0_xattn_a1_wq, L0_xattn_a1_wk, L0_xattn_a1_wv, L0_xattn_a1_wo, L0_xattn_a1_bo, L0_xattn_a2_wq, L0_xattn_a2_wk, L0_xattn_a2_wv, L0_xattn_a2_wo, L0_xattn_a2_bo, L0_xattn_ff_w1, L0_xattn_ff_b1, L0_xattn_ff_w2, L0_xattn_ff_b2, L0_xattn_ln1_g, L0_xattn_ln1_b, L0_xattn_ln2_g, L0_xattn_ln2_b, L0_xattn_ln3_g, L0_xattn_ln3_b)
    x = _L1_xattn_ref(x, ctx_2048, fside_S_0, L1_xattn_W_q, L1_xattn_W_k, L1_xattn_W_v, L1_xattn_W_k_ip, L1_xattn_W_v_ip, L1_xattn_W_out, L1_xattn_b_out)
    return x

_drawn_inputs = setup_inputs


def setup_inputs(seed=0):
    import zlib

    import numpy as np

    out = dict(_drawn_inputs(seed))
    spreads = {'L0_xattn_a1_bo': (0.0, 0.1),
     'L0_xattn_a2_bo': (0.0, 0.1),
     'L0_xattn_ff_b1': (0.0, 0.8),
     'L0_xattn_ff_b2': (0.0, 0.1),
     'L0_xattn_ln1_g': (1.0, 0.6),
     'L0_xattn_ln1_b': (0.0, 0.502),
     'L0_xattn_ln2_g': (1.0, 0.6),
     'L0_xattn_ln2_b': (0.0, 0.8),
     'L0_xattn_ln3_g': (1.0, 0.6),
     'L0_xattn_ln3_b': (0.0, 0.8),
     'L1_xattn_b_out': (0.0, 0.1)}
    factors = {'L0_xattn_a1_wq': 8.0,
     'L0_xattn_a1_wk': 8.0,
     'L0_xattn_a2_wq': 8.0,
     'L0_xattn_a2_wk': 8.0,
     'L0_xattn_ff_w1': 2.954,
     'L0_xattn_ff_w2': 2.931}
    for name, (base, spread) in spreads.items():
        noise = np.random.default_rng([zlib.crc32(name.encode()), seed]).standard_normal(out[name].shape)
        drawn = base * np.exp(spread * noise) if base else spread * noise
        out[name] = jnp.asarray(drawn.astype(out[name].dtype))
    for name, factor in factors.items():
        out[name] = (out[name] * factor).astype(out[name].dtype)
    return out
```

```python
import concourse.bass as bass
from concourse import mybir
from contextlib import ExitStack



def xattn_program(nc: bass.Bass, D, out: bass.AP):
    fp32 = mybir.dt.float32
    f32r = mybir.dt.float32r
    ALU = mybir.AluOpType
    ACT = mybir.ActivationFunctionType
    AX = mybir.AxisListType.X

    x_dram, ctx_dram = D["x"], D["ctx_2048"]
    B, N, C = x_dram.shape
    T, E = ctx_dram.shape[1:]
    H, DH = 20, 64
    INNER = H * DH
    FF = 4 * C
    GB = 4
    GROUPS = B // GB
    NP = H // 2
    U0 = NP * 2
    M = C - 128
    NIP = 4
    TT = T - NIP
    TS = T + NIP + 1
    D1 = C // H
    GS = TT + NIP + 1
    GV = GS + 2 * D1
    W1 = 5
    U1 = GB * W1
    SCALE0, SCALE1 = DH ** -0.5, D1 ** -0.5
    SEM_SCALE, EPS_LN, EPS_L2 = 0.5, 1e-5, 1e-12
    K0 = [N, T]

    JOBS = []

    def ln_jobs(k):
        JOBS.extend([("xT", k, 0), ("xT", k, 1)])

    def pair_jobs(a, p):
        JOBS.extend([("q", a, p), ("k", a, p), ("v", a, p)])

    JOBS.extend([("cT", 0), ("cT", 1)])
    for a in range(2):
        ln_jobs(a)
        for p in range(NP):
            pair_jobs(a, p)
    ln_jobs(2)
    for t in range(FF // 128):
        JOBS.extend([("gate", t), ("up", t)])
    JOBS.extend(("down", b) for b in range(GB))
    ln_jobs(3)
    JOBS.extend([("q1", 0), ("q1", 1), ("k1", 0), ("k1", 1)])
    JOBS.append(("vip", 0))

    def context_jobs(b):
        JOBS.extend([("gram", b), ("v1", b), ("vbd", b)])

    def tail_jobs(b):
        JOBS.extend([("ipT", b), ("ip", b), ("oT1", b), ("y", b)])

    context_jobs(0)
    for b in range(1, GB):
        context_jobs(b)
        tail_jobs(b - 1)
    tail_jobs(GB - 1)
    JOB = {name: n for n, name in enumerate(JOBS)}

    def read_out(name):
        kind, i = name[0], name[-1]
        if kind == "xT":
            return "nT_dve", 2 * name[1] + i + 1
        if kind in "qkv":
            return kind + "_done", NP * name[1] + i + 1
        return {"cT": "cT_dve", "gate": "gelu_done", "up": "h_done", "down": "down_added", "q1": "q1_done",
                "k1": "kbd_done", "vip": "vip_done", "gram": "gram_done", "v1": "gv_done", "vbd": "vbd_done",
                "ipT": "ipT_done", "ip": "o1_done", "oT1": "o1T_done", "y": "y_done"}[kind], i + 1

    ctx = ExitStack()
    with ctx:
        def sb(name, shape, dt=fp32):
            return ctx.enter_context(nc.sbuf_tensor(name, shape, dt))

        def split_weights(name, n):
            return (sb(name + "_hi", [128, n], f32r), sb(name + "_lo", [128, n], f32r),
                    sb(name + "_rem", [128, n], f32r))

        w_q = [split_weights("w_q0", INNER), split_weights("w_q1", INNER)]
        w_k0 = split_weights("w_k0", INNER)
        w_v0 = split_weights("w_v0", INNER)
        w_kc = sb("w_kc", [128, 2, 2, INNER], f32r)
        w_vc = sb("w_vc", [128, 2, 2, INNER], f32r)
        w_o = [sb("w_o0", [128, NP, C]), sb("w_o1", [128, NP, C])]
        w_1 = split_weights("w_1", 2 * FF)
        w_2 = sb("w_2", [128, FF // 128, C])
        w_q1 = split_weights("w_q1h", C)
        w_k1 = sb("w_k1h", [128, 2, 2, C], f32r)
        w_v1 = sb("w_v1h", [128, 2, 2, C], f32r)
        w_kip = sb("w_kip", [128, 2, C])
        w_vip = sb("w_vip", [128, 2, C])
        w_out = sb("w_out", [128, C])
        w_out_rem = sb("w_out_rem", [128, C])
        ln_g = sb("ln_g", [128, 3, C])
        ln_b = sb("ln_b", [128, 3, C])
        bias = sb("bias", [128, 4, C])
        b_1 = sb("b_1", [128, 2 * FF // 128])
        fside = sb("fside", [128, 1])
        ident = sb("ident", [128, 128])
        is_ip = sb("is_ip", [TS, 1])
        not_ip = sb("not_ip", [TS, 1])
        head_of_row = sb("head_of_row", [128, 4])
        own16 = sb("own16", [128, 16])
        own_head = sb("own_head", [H * NIP, H, D1])
        pick = sb("pick", [GB * NIP, GB, H * NIP])
        p_half = sb("p_half", [128, H])
        p_mhalf = sb("p_mhalf", [128, GB])
        xin = sb("xin", [128, GB, C])
        xres = sb("xres", [128, GB, C])
        cin = sb("cin", [TS, GB, E])
        cT = sb("cT", [128, 2, 2, GB * TS], f32r)
        cipT = sb("cipT", [128, 2, GB * NIP])
        cst = sb("cst", [TS, 4, GB])
        nT = sb("nT", [128, 3, GB * 128], f32r)
        st6 = sb("st6", [128, GB, 6])
        mv = sb("mv", [128, GB, 2])
        rstd = sb("rstd", [128, GB])
        vp = sb("vp", [128, GB])
        qk = sb("qk", [128, 6, 512])
        v_sb = sb("v_sb", [128, 2, GB, 2, DH + 1])
        SE = sb("SE", [128, 3, 512])
        PTs = sb("PTs", [128, 2, 512])
        work = sb("work", [128, 1024])
        ON = work[:, 0:512].rearrange("p (i n) -> p i n", i=2)
        OTs = work[:, 512:1024].rearrange("p (i n) -> p i n", i=2)
        mx = sb("mx", [128, 2, 4])
        rs = sb("rs", [128, 2, 4])
        hT = sb("hT", [128, FF // 128, 512])
        SE_flat = SE[:, :, :].rearrange("p i n -> p (i n)")
        lt = SE_flat[:, 0:GB * C].rearrange("p (b c) -> p b c", b=GB)
        csq = SE_flat[0:TS, GB * C:GB * C + E]
        gl = SE[:, 0:2, :]
        nx = hT[:, 0:2, :].rearrange("p i (h n) -> p (i h) n", h=2)
        q1T = hT[:, 2:4, :]
        kbd = qk[:, :, :].rearrange("p i n -> p (i n)")[:, 0:2 * GB * 4 * T]\
            .rearrange("p (r b h t) -> p r b h t", r=2, b=GB, h=4)
        gp = work[:, 0:4 * TT].rearrange("p (i t) -> p i t", i=4)
        ipTs = work[0:H * NIP, 292:420]
        o1T = work[:, 420:676]
        sem4 = work[:, 676:836].rearrange("p (k h n) -> p k h n", k=2, h=H)
        o1b = work[:, 836:996]
        yo = xin
        vip_sb = sb("vip_sb", [GB * NIP, C])
        vbd_sb = sb("vbd_sb", [H * NIP, 2, H, D1])
        gv = sb("gv", [TT, 2, NP, GV])
        sip = sb("sip", [128, 2, H, NIP])
        qq = sb("qq", [128, 2, H])
        rr = sb("rr", [128, 2, H])
        r20 = sb("r20", [128, 4, H])
        o1 = sb("o1", [128, 2, H, D1])

        PG = [ctx.enter_context(nc.psum_tensor(f"PG{i}", [128, 512], fp32)) for i in range(2)]
        PS = [ctx.enter_context(nc.psum_tensor(f"PS{i}", [128, 512], fp32)) for i in range(2)]
        PT = ctx.enter_context(nc.psum_tensor("PT", [128, 512], fp32))
        PV = ctx.enter_context(nc.psum_tensor("PV", [128, 512], fp32))
        PO = ctx.enter_context(nc.psum_tensor("PO", [128, 512], fp32))
        PW = ctx.enter_context(nc.psum_tensor("PW", [128, 512], fp32))

        def sem(name):
            return ctx.enter_context(nc.semaphore(name))

        stage_in = [sem("stage_in0"), sem("stage_in1")]
        stage_used = sem("stage_used")
        plain_in = sem("plain_in")
        setup_dve = sem("setup_dve")
        setup_pool = sem("setup_pool")

        SPLITS = []
        for name, tiles in (("L0_xattn_a1_wq", w_q[0]), ("L0_xattn_a1_wk", w_k0), ("L0_xattn_a1_wv", w_v0),
                            ("L0_xattn_a2_wq", w_q[1]), ("L0_xattn_ff_w1", w_1), ("L1_xattn_W_q", w_q1)):
            n = D[name].shape[1]
            SPLITS.append(([(D[name][0:128, :], 0, 128)], tiles[0][:, :], tiles[1][:, :], n))
            SPLITS.append(([(D[name][128:C, :], M * r, M * r + M) for r in range(4)], tiles[2][:, :], None, n))
        for name, tile in (("L0_xattn_a2_wk", w_kc), ("L0_xattn_a2_wv", w_vc),
                           ("L1_xattn_W_k", w_k1), ("L1_xattn_W_v", w_v1)):
            n = D[name].shape[1]
            for c in range(2):
                SPLITS.append(([(D[name][128 * c:128 * c + 128, :], 0, 128)], tile[:, c, 0, :], tile[:, c, 1, :], n))
        stage = [hT[:, 0:3, :].rearrange("p a b -> p (a b)"), qk[:, 0:3, :].rearrange("p a b -> p (a b)")]

        PLAIN = []
        for a, w in enumerate(("L0_xattn_a1_wo", "L0_xattn_a2_wo")):
            PLAIN.append((w_o[a][:, :, :], D[w].rearrange("(p k) n -> k p n", k=128)))
        PLAIN.append((w_2[:, :, :], D["L0_xattn_ff_w2"].rearrange("(p k) n -> k p n", k=128)))
        for w, t in (("L1_xattn_W_k_ip", w_kip), ("L1_xattn_W_v_ip", w_vip)):
            PLAIN.append((t[:, :, :], D[w].rearrange("(c k) n -> k c n", k=128)))
        PLAIN.append((w_out[:, :], D["L1_xattn_W_out"][0:128, :]))
        PLAIN.append((w_out_rem[96:128, :], D["L1_xattn_W_out"][128:C, :]))
        for k in range(3):
            PLAIN.append((ln_g[:, k, :], D[f"L0_xattn_ln{k + 1}_g"].partition_broadcast(128)))
            PLAIN.append((ln_b[:, k, :], D[f"L0_xattn_ln{k + 1}_b"].partition_broadcast(128)))
        for k, w in enumerate(("L0_xattn_a1_bo", "L0_xattn_a2_bo", "L0_xattn_ff_b2", "L1_xattn_b_out")):
            PLAIN.append((bias[:, k, :], D[w].partition_broadcast(128)))
        PLAIN.append((b_1[:, :], D["L0_xattn_ff_b1"].rearrange("(t p) -> p t", p=128)))
        PLAIN.append((fside[:, :], D["fside_S_0"].rearrange("(p a) -> p a", a=1)))

        with nc.Block() as block:
            @block.sync
            def _(sp):
                count = [0, 0]
                for i, (parts, _, _, n) in enumerate(SPLITS):
                    if i >= 2:
                        sp.wait_ge(stage_used, i - 1)
                    for src, p0, p1 in parts:
                        sp.dma_start(stage[i % 2][p0:p1, 0:n], src).then_inc(stage_in[i % 2], 16)

            @block.scalar
            def _(act):
                for dst, src in PLAIN:
                    act.dma_start(dst, src, allow_slow_non_contiguous=True).then_inc(plain_in, 16)
                act.wait_ge(plain_in, 16 * len(PLAIN))

            @block.vector
            def _(dve):
                count = [0, 0]
                steps = 0
                for i, (parts, hi, lo, n) in enumerate(SPLITS):
                    count[i % 2] += 16 * len(parts)
                    dve.wait_ge(stage_in[i % 2], count[i % 2])
                    s = stage[i % 2]
                    nc.vector.tensor_copy(hi, s[:, 0:n]).then_inc(setup_dve, 1)
                    steps += 1
                    dve.wait_ge(setup_dve, steps)
                    if lo is not None:
                        nc.vector.tensor_tensor(lo, s[:, 0:n], hi.bitcast(fp32), ALU.subtract).then_inc(stage_used, 1)
                    else:
                        nc.vector.tensor_tensor(hi[M:2 * M], s[M:2 * M, 0:n], hi[M:2 * M].bitcast(fp32), ALU.subtract)
                        nc.vector.tensor_tensor(hi[3 * M:4 * M], s[3 * M:4 * M, 0:n], hi[3 * M:4 * M].bitcast(fp32),
                                                ALU.subtract).then_inc(stage_used, 1)
                dve.wait_ge(stage_used, len(SPLITS))
                nc.vector.memset(v_sb[:, :, :, :, :], 1.0)
                nc.vector.memset(gv[:, :, :, :], 1.0)

            @block.gpsimd
            def _(pool):
                g = nc.gpsimd
                steps = [0]

                def done(ins):
                    steps[0] += 1
                    ins.then_inc(setup_pool, 1)
                    pool.wait_ge(setup_pool, steps[0])

                g.memset(p_half[:, :], 0.5)
                g.memset(p_mhalf[:, :], -0.5)
                done(g.memset(cin[:, :, :], 0.0))
                done(g.memset(ident[:, :], 0.0))
                done(g.affine_select(out=ident[:, :], in_=ident[:, :], compare_op=ALU.not_equal, fill=1.0,
                                     base=0, pattern=[[-1, 128]], channel_multiplier=1))
                done(g.memset(is_ip[:, :], 1.0))
                done(g.affine_select(out=is_ip[:, :], in_=is_ip[:, :], compare_op=ALU.is_ge, fill=0.0,
                                     base=-T, pattern=[[0, 1]], channel_multiplier=1))
                done(g.tensor_scalar(not_ip[:, :], is_ip[:, :], -1.0, 1.0, ALU.mult, ALU.add))
                done(g.memset(own16[:, :], 1.0))
                done(g.affine_select(out=own16[:, :], in_=own16[:, :], compare_op=ALU.is_ge, fill=0.0,
                                     base=0, pattern=[[-D1, 16]], channel_multiplier=1))
                done(g.affine_select(out=own16[:, :], in_=own16[:, :], compare_op=ALU.is_ge, fill=0.0,
                                     base=D1 - 1, pattern=[[D1, 16]], channel_multiplier=-1))
                done(g.tensor_tensor(head_of_row[:, :], own16[:, 0:4], own16[:, 4:8], ALU.add))
                done(g.tensor_tensor(head_of_row[:, :], head_of_row[:, :], own16[:, 8:12], ALU.add))
                done(g.tensor_tensor(head_of_row[:, :], head_of_row[:, :], own16[:, 12:16], ALU.add))
                done(g.memset(own_head[:, :, :], 1.0))
                done(g.affine_select(out=own_head[:, :, :], in_=own_head[:, :, :], compare_op=ALU.is_ge, fill=0.0,
                                     base=0, pattern=[[-NIP, H], [0, D1]], channel_multiplier=1))
                done(g.affine_select(out=own_head[:, :, :], in_=own_head[:, :, :], compare_op=ALU.is_ge, fill=0.0,
                                     base=NIP - 1, pattern=[[NIP, H], [0, D1]], channel_multiplier=-1))
                pk = pick[:, :, :].rearrange("p b (h n) -> p b h n", n=NIP)
                done(g.memset(pick[:, :, :], 0.0))
                done(g.affine_select(out=pk, in_=pk, compare_op=ALU.not_equal, fill=1.0, base=0,
                                     pattern=[[-NIP, GB], [0, H], [-1, NIP]], channel_multiplier=1))

        names = ["x_in", "c_in", "out_done",
                 "job_full", "down_added", "gram_done",
                 "ln_stats", "ln_t", "rstd_done", "nx_done", "nT_act", "nT_dve", "k_zero", "bias_added",
                 "c_sq", "c_pow", "c_dve", "cT_act", "cT_dve",
                 "q_done", "k_done", "v_done",
                 "s_done", "mx_done", "sub_done", "exp_done", "pt_done", "pts_done", "pv_done", "rs_done",
                 "on_done", "ot_done", "ots_done", "wo_done", "x_done",
                 "gelu_done", "h_done",
                 "q1_done", "kbd_done", "vip_done", "vbd_done", "gv_done",
                 "sip_done", "gp_done", "qq_done", "n20_done", "d_chain", "sipe_done", "mask_done", "ipT_done", "o1_done",
                 "o1T_done", "y_done", "pool_c"]
        S = {n: sem(n) for n in names}
        nums = sorted(s.num for s in S.values())
        assert nums == list(range(nums[0], nums[0] + len(nums)))

        def bank(name):
            return PG[JOB[name] % 2]

        with nc.Fori(0, GROUPS) as grp:
            with nc.Block() as block:
                xg = x_dram.rearrange("(g b) n c -> g n b c", b=GB)
                cg = ctx_dram.rearrange("(g b) t e -> g t b e", b=GB)
                og = out.rearrange("(g b) n c -> g b n c", b=GB)

                @block.sync
                def _(sp):
                    sp.dma_start(xin[:, :, :], xg[grp, :, :, :]).then_inc(S["x_in"], 16)
                    sp.dma_start(cin[0:T, :, :], cg[grp, :, :, :]).then_inc(S["c_in"], 16)
                    sp.dma_start(cin[T:T + NIP, :, :], cg[grp, TT:T, :, :]).then_inc(S["c_in"], 16)
                    for b in range(GB):
                        sp.wait_ge(S["y_done"], b + 1)
                        sp.dma_start(og[grp, b, :, :], yo[:, b, :]).then_inc(S["out_done"], 16)
                    sp.wait_ge(S["out_done"], 16 * GB)

                @block.tensor
                def _(pe):
                    mm = nc.tensor.matmul

                    def open_job(name):
                        if JOB[name] >= 2:
                            which, count = read_out(JOBS[JOB[name] - 2])
                            pe.wait_ge(S[which], count)
                        return bank(name)

                    def transposed_input(k):
                        ps = open_job(("xT", k, 0))
                        pe.wait_ge(S["nx_done"], 2 * GB * (k + 1))
                        for part in range(2):
                            if part:
                                ps = open_job(("xT", k, 1))
                            for b in range(GB):
                                last = nc.tensor.transpose(ps[:, 128 * b:128 * b + 128],
                                                           nx[:, b, 128 * part:128 * part + 128], ident[:, :])
                            last.then_inc(S["job_full"], 1)

                    def wait_nT(k):
                        pe.wait_ge(S["nT_act"], 2 * (k + 1))
                        pe.wait_ge(S["nT_dve"], 2 * (k + 1))

                    def rows160(ps, w, c0, cols=slice(0, GB * 128)):
                        mm(ps, w[0][:, c0:c0 + 128], nT[:, 0, cols], start=True, stop=False)
                        mm(ps, w[1][:, c0:c0 + 128], nT[:, 0, cols], start=False, stop=False)
                        mm(ps, w[0][:, c0:c0 + 128], nT[:, 1, cols], start=False, stop=False)
                        return mm(ps, w[2][:, c0:c0 + 128], nT[:, 2, cols], start=False, stop=True)

                    def rows160_out(ps, w, c0, n, b):
                        t = slice(128 * b, 128 * b + 128)
                        mm(ps, nT[:, 0, t], w[0][:, c0:c0 + n], start=True, stop=False)
                        mm(ps, nT[:, 0, t], w[1][:, c0:c0 + n], start=False, stop=False)
                        mm(ps, nT[:, 1, t], w[0][:, c0:c0 + n], start=False, stop=False)
                        return mm(ps, nT[:, 2, t], w[2][:, c0:c0 + n], start=False, stop=True)

                    SPLIT3 = [(0, 0), (0, 1), (1, 0)]

                    def ctx_cols(ps, w, c0, stop=True):
                        for c in range(2):
                            for i, (hw, hc) in enumerate(SPLIT3):
                                last = mm(ps, w[:, c, hw, c0:c0 + 128], cT[:, c, hc, :],
                                          start=(c == 0 and i == 0), stop=(c == 1 and i == 2))
                        return last

                    def ctx_rows(ps, w, c0, n, b, rows):
                        for c in range(2):
                            for i, (hw, hc) in enumerate(SPLIT3):
                                last = mm(ps, cT[:, c, hc, TS * b:TS * b + rows], w[:, c, hw, c0:c0 + n],
                                          start=(c == 0 and i == 0), stop=(c == 1 and i == 2))
                        return last

                    def project_q(a, p):
                        ps = open_job(("q", a, p))
                        rows160(ps[:, :], w_q[a], 128 * p).then_inc(S["job_full"], 1)

                    def project_k(a, p):
                        ps = open_job(("k", a, p))
                        if a == 0:
                            last = rows160(ps[:, :], w_k0, 128 * p)
                        else:
                            last = ctx_cols(ps[:, 0:GB * TS], w_kc, 128 * p)
                        last.then_inc(S["job_full"], 1)

                    def project_v(a, p):
                        ps = open_job(("v", a, p))
                        for b in range(GB):
                            o = ps[0:K0[a], 128 * b:128 * b + 128]
                            if a == 0:
                                last = rows160_out(o, w_v0, 128 * p, 128, b)
                            else:
                                last = ctx_rows(o, w_vc, 128 * p, 128, b, T)
                        last.then_inc(S["job_full"], 1)

                    for c in range(2):
                        ps = open_job(("cT", c))
                        pe.wait_ge(S["c_dve"], 4)
                        for b in range(GB):
                            last = nc.tensor.transpose(ps[:, TS * b:TS * b + TS], cin[:, b, 128 * c:128 * c + 128],
                                                       ident[0:TS, 0:TS])
                        last.then_inc(S["job_full"], 1)

                    for a in range(2):
                        J, U = K0[a], U0 * a
                        transposed_input(a)
                        wait_nT(a)
                        if a == 1:
                            pe.wait_ge(S["cT_act"], 2)
                            pe.wait_ge(S["cT_dve"], 2)
                        project_q(a, 0)
                        project_k(a, 0)
                        project_v(a, 0)
                        for s in range(U0 + 4):
                            if s < U0:
                                u, p, half = U + s, s // 2, s % 2
                                q, ke, ko = (qk[:, 3 * (p % 2) + i, :] for i in range(3))
                                if half == 0:
                                    pe.wait_ge(S["q_done"], NP * a + p + 1)
                                    pe.wait_ge(S["k_done"], NP * a + p + 1)
                                if u >= 2:
                                    pe.wait_ge(S["sub_done"], u - 1)
                                kstep = 128 if a == 0 else TS
                                for i in range(4):
                                    b, k = 2 * half + i // 2, (ke, ko)[i % 2]
                                    last = mm(PS[u % 2][:, J * i:J * i + J], q[:, 128 * b:128 * b + 128],
                                              k[:, kstep * b:kstep * b + J], start=True, stop=True)
                                last.then_inc(S["s_done"], 1)
                                if half == 0 and p + 1 < NP:
                                    project_q(a, p + 1)
                                if half == 1 and p + 1 < NP:
                                    project_k(a, p + 1)
                            if 0 <= s - 1 < U0:
                                u = U + s - 1
                                pe.wait_ge(S["exp_done"], u + 1)
                                if u >= 1:
                                    pe.wait_ge(S["pts_done"], u)
                                for i in range(4):
                                    last = nc.tensor.transpose(PT[0:J, 128 * i:128 * i + 128],
                                                               SE[:, u % 3, J * i:J * i + J], ident[:, :])
                                last.then_inc(S["pt_done"], 1)
                            if 0 <= s - 2 < U0:
                                u, p, half = U + s - 2, (s - 2) // 2, s % 2
                                pe.wait_ge(S["pts_done"], u + 1)
                                pe.wait_ge(S["v_done"], NP * a + p + 1)
                                if u >= 1:
                                    pe.wait_ge(S["on_done"], u)
                                for i in range(4):
                                    last = mm(PV[:, (DH + 1) * i:(DH + 1) * (i + 1)],
                                              PTs[0:J, u % 2, 128 * i:128 * i + 128],
                                              v_sb[0:J, p % 2, 2 * half + i // 2, i % 2, :], start=True, stop=True)
                                last.then_inc(S["pv_done"], 1)
                            if s < U0 and s % 2 == 1 and s // 2 + 1 < NP:
                                project_v(a, s // 2 + 1)
                            if 0 <= s - 3 < U0:
                                u = U + s - 3
                                pe.wait_ge(S["on_done"], u + 1)
                                if u >= 1:
                                    pe.wait_ge(S["ots_done"], u)
                                for i in range(2):
                                    last = nc.tensor.transpose(PO[:, 128 * i:128 * i + 128],
                                                               ON[:, u % 2, 128 * i:128 * i + 128], ident[:, :])
                                last.then_inc(S["ot_done"], 1)
                            if 0 <= s - 4 < U0:
                                u, p = U + s - 4, (s - 4) // 2
                                pe.wait_ge(S["ots_done"], u + 1)
                                if u >= 1:
                                    pe.wait_ge(S["x_done"], u)
                                for i in range(2):
                                    last = mm(PW[:, C * i:C * i + C], OTs[:, u % 2, 128 * i:128 * i + 128],
                                              w_o[a][:, p, :], start=True, stop=True)
                                last.then_inc(S["wo_done"], 1)

                    transposed_input(2)
                    wait_nT(2)
                    for t in range(FF // 128):
                        ps = open_job(("gate", t))
                        rows160(ps[:, :], w_1, FF + 128 * t).then_inc(S["job_full"], 1)
                        ps = open_job(("up", t))
                        rows160(ps[:, :], w_1, 128 * t).then_inc(S["job_full"], 1)
                    for b in range(GB):
                        ps = open_job(("down", b))
                        for t in range(FF // 128):
                            pe.wait_ge(S["h_done"], t + 1)
                            last = mm(ps[:, 0:C], hT[:, t, 128 * b:128 * b + 128], w_2[:, t, :],
                                      start=(t == 0), stop=(t == FF // 128 - 1))
                        last.then_inc(S["job_full"], 1)

                    transposed_input(3)
                    wait_nT(3)
                    for r in range(2):
                        ps = open_job(("q1", r))
                        rows160(ps[:, :], w_q1, M * r).then_inc(S["job_full"], 1)
                    for r in range(2):
                        ps = open_job(("k1", r))
                        ctx_cols(ps[:, 0:GB * TS], w_k1, M * r)
                        for c in range(2):
                            last = mm(ps[:, GB * TS:GB * TS + GB * NIP], w_kip[:, c, M * r:M * r + 128], cipT[:, c, :],
                                      start=(c == 0), stop=(c == 1))
                        last.then_inc(S["job_full"], 1)
                    ps = open_job(("vip", 0))
                    for c in range(2):
                        last = mm(ps[0:GB * NIP, 0:C], cipT[:, c, :], w_vip[:, c, :], start=(c == 0), stop=(c == 1))
                    last.then_inc(S["job_full"], 1)

                    def l1_context(b):
                        ps = open_job(("gram", b))
                        for c in range(2):
                            for i, (h0, h1) in enumerate(SPLIT3):
                                last = mm(ps[0:TT, 0:TS], cT[:, c, h0, TS * b:TS * b + TT], cT[:, c, h1, TS * b:TS * b + TS],
                                          start=(c == 0 and i == 0), stop=(c == 1 and i == 2))
                        last.then_inc(S["job_full"], 1)
                        ps = open_job(("v1", b))
                        ctx_rows(ps[0:TT, 0:C], w_v1, 0, C, b, TT).then_inc(S["job_full"], 1)
                        ps = open_job(("vbd", b))
                        pe.wait_ge(S["vip_done"], 1)
                        mm(ps[0:H * NIP, 0:C], pick[:, b, :], vip_sb[:, :], start=True, stop=True).then_inc(S["job_full"], 1)

                    def l1_tail(b):
                        ps = open_job(("ipT", b))
                        pe.wait_ge(S["mask_done"], b + 1)
                        nc.tensor.transpose(ps[0:H * NIP, 0:128], sip[:, b % 2, :, :].rearrange("p h n -> p (h n)"),
                                            ident[:, :]).then_inc(S["job_full"], 1)
                        ps = open_job(("ip", b))
                        pe.wait_ge(S["ipT_done"], b + 1)
                        pe.wait_ge(S["vbd_done"], b + 1)
                        mm(ps[:, 0:C], ipTs, vbd_sb[:, b % 2, :, :].rearrange("p h d -> p (h d)"),
                           start=True, stop=True).then_inc(S["job_full"], 1)
                        ps = open_job(("oT1", b))
                        pe.wait_ge(S["o1_done"], b + 1)
                        nc.tensor.transpose(ps[:, 0:128], o1b[:, 0:128], ident[:, :])
                        nc.tensor.transpose(ps[:, 128:256], o1b[:, M:C], ident[:, :]).then_inc(S["job_full"], 1)
                        ps = open_job(("y", b))
                        pe.wait_ge(S["o1T_done"], b + 1)
                        mm(ps[:, 0:C], o1T[:, 0:128], w_out[:, :], start=True, stop=False)
                        mm(ps[:, 0:C], o1T[96:128, 128:256], w_out_rem[96:128, :], start=False, stop=True).then_inc(S["job_full"], 1)

                    UB = 2 * U0
                    pe.wait_ge(S["q1_done"], 2)
                    pe.wait_ge(S["kbd_done"], 2)
                    for s in range(U1 + 2):
                        if s < U1:
                            u, b, w = UB + s, s // W1, s % W1
                            if w == 0:
                                l1_context(b)
                            pe.wait_ge(S["sub_done"], u - 1)
                            r, row = (0, 32 * w) if w < 4 else (1, 96)
                            mm(PS[u % 2][:, 0:4 * T], q1T[row:row + 32, r, 128 * b:128 * b + 128],
                               kbd[row:row + 32, r, b, :, :].rearrange("p h t -> p (h t)"),
                               start=True, stop=True).then_inc(S["s_done"], 1)
                        if 0 <= s - 1 < U1:
                            u = UB + s - 1
                            pe.wait_ge(S["exp_done"], u + 1)
                            pe.wait_ge(S["pts_done"], u)
                            for i in range(4):
                                last = nc.tensor.transpose(PT[0:TT, 128 * i:128 * i + 128],
                                                           SE[:, u % 3, TT * i:TT * i + TT], ident[:, :])
                            last.then_inc(S["pt_done"], 1)
                        if 0 <= s - 2 < U1:
                            u, b, w = UB + s - 2, (s - 2) // W1, (s - 2) % W1
                            pe.wait_ge(S["pts_done"], u + 1)
                            pe.wait_ge(S["gv_done"], b + 1)
                            pe.wait_ge(S["on_done"], u)
                            for i in range(4):
                                off = D1 * (i % 2)
                                last = mm(PV[:, GV * i + off:GV * i + off + GS + D1],
                                          PTs[0:TT, u % 2, 128 * i:128 * i + 128],
                                          gv[:, b % 2, 2 * w + i // 2, off:off + GS + D1], start=True, stop=True)
                            last.then_inc(S["pv_done"], 1)
                            if w == 2 and b >= 1:
                                l1_tail(b - 1)
                    l1_tail(GB - 1)

                @block.scalar
                def _(act):
                    a_ = nc.scalar.activation

                    def take(name):
                        act.wait_ge(S["job_full"], JOB[name] + 1)
                        return bank(name)

                    def input_hi(k):
                        ps = take(("xT", k, 0))
                        a_(nT[:, 0, :], ps[:, :], ACT.Copy).then_inc(S["nT_act"], 1)
                        ps = take(("xT", k, 1))
                        a_(nT[:, 2, :], ps[:, :], ACT.Copy).then_inc(S["nT_act"], 1)

                    act.wait_ge(S["c_in"], 32)
                    for b in range(GB):
                        if b:
                            act.wait_ge(S["c_sq"], b)
                        a_(csq, cin[:, b, :], ACT.Square, accum_out=cst[:, 0, b:b + 1]).then_inc(S["c_sq"], 1)
                    for c in range(2):
                        ps = take(("cT", c))
                        a_(cT[:, c, 0, :], ps[:, 0:GB * TS], ACT.Copy).then_inc(S["cT_act"], 1)

                    def exp_unit(u, cols, scale):
                        act.wait_ge(S["sub_done"], u + 1)
                        a_(SE[:, u % 3, 0:cols], SE[:, u % 3, 0:cols], ACT.Exp, scale=scale).then_inc(S["exp_done"], 1)

                    def pt_out(u, J):
                        act.wait_ge(S["pt_done"], u + 1)
                        if u >= 2:
                            act.wait_ge(S["pv_done"], u - 1)
                        a_(PTs[0:J, u % 2, :], PT[0:J, :], ACT.Copy).then_inc(S["pts_done"], 1)

                    for a in range(2):
                        J, U = K0[a], U0 * a
                        kw = 512 if a == 0 else GB * TS
                        input_hi(a)

                        def q_take(p):
                            ps = take(("q", a, p))
                            a_(qk[:, 3 * (p % 2), :], ps[:, :], ACT.Copy).then_inc(S["q_done"], 1)

                        def k_take(p):
                            ps = take(("k", a, p))
                            if a == 0 and p == 0:
                                act.wait_ge(S["k_zero"], 4)
                            a_(qk[0:DH, 3 * (p % 2) + 1, 0:kw], ps[0:DH, 0:kw], ACT.Copy)
                            a_(qk[DH:128, 3 * (p % 2) + 2, 0:kw], ps[DH:128, 0:kw], ACT.Copy).then_inc(S["k_done"], 1)

                        q_take(0)
                        k_take(0)
                        for s in range(U0 + 4):
                            if s < U0:
                                exp_unit(U + s, 4 * J, SCALE0)
                                p = s // 2
                                if p + 1 < NP:
                                    (q_take if s % 2 == 0 else k_take)(p + 1)
                            if 0 <= s - 1 < U0:
                                pt_out(U + s - 1, J)
                            if 0 <= s - 3 < U0:
                                u = U + s - 3
                                act.wait_ge(S["ot_done"], u + 1)
                                if u >= 2:
                                    act.wait_ge(S["wo_done"], u - 1)
                                a_(OTs[:, u % 2, :], PO[:, 0:256], ACT.Copy).then_inc(S["ots_done"], 1)

                    input_hi(2)
                    for t in range(FF // 128):
                        ps = take(("gate", t))
                        if t >= 2:
                            act.wait_ge(S["h_done"], t - 1)
                        a_(gl[:, t % 2, :], ps[:, :], ACT.Gelu, bias=b_1[:, FF // 128 + t:FF // 128 + t + 1])\
                            .then_inc(S["gelu_done"], 1)

                    input_hi(3)
                    for r in range(2):
                        ps = take(("q1", r))
                        a_(q1T[:, r, :], ps[:, :], ACT.Copy).then_inc(S["q1_done"], 1)

                    def l1_tail_exp(b):
                        act.wait_ge(S["sip_done"], b + 1)
                        a_(sip[:, b % 2, :, :], sip[:, b % 2, :, :], ACT.Exp).then_inc(S["sipe_done"], 1)

                    def l1_tail_copies(b):
                        ps = take(("ipT", b))
                        if b:
                            act.wait_ge(S["job_full"], JOB[("ip", b - 1)] + 1)
                        a_(ipTs, ps[0:H * NIP, 0:128], ACT.Copy).then_inc(S["ipT_done"], 1)
                        ps = take(("oT1", b))
                        a_(o1T, ps[:, 0:256], ACT.Copy).then_inc(S["o1T_done"], 1)

                    UB = 2 * U0
                    for s in range(U1 + 2):
                        if s < U1:
                            exp_unit(UB + s, 4 * TT, SCALE1)
                        if 0 <= s - 1 < U1:
                            pt_out(UB + s - 1, TT)
                        if 0 <= s - 2 < U1 and (s - 2) % W1 == 1 and (s - 2) // W1 >= 1:
                            l1_tail_exp((s - 2) // W1 - 1)
                        if 0 <= s - 2 < U1 and (s - 2) % W1 == 2 and (s - 2) // W1 >= 1:
                            l1_tail_copies((s - 2) // W1 - 1)
                    l1_tail_exp(GB - 1)
                    l1_tail_copies(GB - 1)

                @block.vector
                def _(dve):
                    v = nc.vector
                    chain = [0]

                    def then(ins):
                        chain[0] += 1
                        ins.then_inc(S["d_chain"], 1)
                        dve.wait_ge(S["d_chain"], chain[0])

                    def take(name):
                        dve.wait_ge(S["job_full"], JOB[name] + 1)
                        return bank(name)

                    def layer_norm(k, src):
                        for b in range(GB):
                            last = v.bn_stats(st6[:, b, :], src[:, b, :])
                        then(last)
                        for b in range(GB):
                            last = v.bn_aggr(mv[:, b, :], st6[:, b, :])
                        last.then_inc(S["ln_stats"], 1)
                        dve.wait_ge(S["ln_stats"], k + 1)
                        for b in range(GB):
                            last = v.scalar_tensor_tensor(lt[:, b, :], src[:, b, :], mv[:, b, 0:1], ln_g[:, k, :],
                                                          ALU.subtract, ALU.mult)
                        last.then_inc(S["ln_t"], 1)
                        dve.wait_ge(S["ln_t"], k + 1)
                        dve.wait_ge(S["rstd_done"], k + 1)
                        rest = lambda ap: ap[:, 128:C].unsqueeze(1).to_broadcast([128, 4, M])
                        for b in range(GB):
                            v.scalar_tensor_tensor(nx[:, b, 0:128], lt[:, b, 0:128], rstd[:, b:b + 1], ln_b[:, k, 0:128],
                                                   ALU.mult, ALU.add).then_inc(S["nx_done"], 1)
                            v.scalar_tensor_tensor(nx[:, b, 128:256].rearrange("p (r m) -> p r m", m=M),
                                                   rest(lt[:, b, :]), rstd[:, b:b + 1], rest(ln_b[:, k, :]),
                                                   ALU.mult, ALU.add).then_inc(S["nx_done"], 1)

                    def input_lo(k):
                        ps = take(("xT", k, 0))
                        dve.wait_ge(S["nT_act"], 2 * k + 1)
                        v.tensor_tensor(nT[:, 1, :], ps[:, :], nT[:, 0, :].bitcast(fp32),
                                        ALU.subtract).then_inc(S["nT_dve"], 1)
                        ps = take(("xT", k, 1))
                        dve.wait_ge(S["nT_act"], 2 * k + 2)
                        v.tensor_tensor(nT[64:128, 2, :], ps[64:128, :], nT[64:128, 2, :].bitcast(fp32),
                                        ALU.subtract).then_inc(S["nT_dve"], 1)

                    dve.wait_ge(S["pool_c"], 1)
                    then(v.tensor_scalar(cst[:, 2, :], cst[:, 1, :], EPS_L2, None, ALU.max))
                    then(v.reciprocal(cst[:, 3, :], cst[:, 2, :]))
                    then(v.tensor_scalar(cst[:, 2, :], cst[:, 3, :], is_ip[:, 0:1], not_ip[:, 0:1], ALU.mult, ALU.add))
                    for b in range(GB):
                        v.tensor_scalar(cin[:, b, :], cin[:, b, :], cst[:, 2, b:b + 1], None, ALU.mult)\
                            .then_inc(S["c_dve"], 1)

                    def ctx_lo(c):
                        ps = take(("cT", c))
                        dve.wait_ge(S["cT_act"], c + 1)
                        v.tensor_tensor(cT[:, c, 1, :], ps[:, 0:GB * TS], cT[:, c, 0, :].bitcast(fp32), ALU.subtract)
                        ip = ps[:, 0:GB * TS].rearrange("p (b t) -> p b t", t=TS)[:, :, TT:T]
                        v.tensor_copy(cipT[:, c, :].rearrange("p (b n) -> p b n", n=NIP), ip)\
                            .then_inc(S["cT_dve"], 1)

                    dve.wait_ge(S["x_in"], 16)
                    for c in range(2):
                        ctx_lo(c)

                    def softmax_in(u, n, cols, step):
                        dve.wait_ge(S["s_done"], u + 1)
                        sc = PS[u % 2][:, 0:n * step].rearrange("p (i j) -> p i j", j=step)[:, :, 0:cols]
                        v.tensor_reduce(mx[:, u % 2, :], sc, AX, ALU.max).then_inc(S["mx_done"], 1)
                        dve.wait_ge(S["mx_done"], u + 1)
                        if u >= 3:
                            dve.wait_ge(S["pt_done"], u - 2)
                        m = mx[:, u % 2, :].unsqueeze(2).to_broadcast([128, n, cols])
                        return sc, v.tensor_tensor(SE[:, u % 3, 0:n * cols].rearrange("p (i j) -> p i j", j=cols), sc, m,
                                                   ALU.subtract)

                    def unit_out(u):
                        dve.wait_ge(S["pv_done"], u + 1)
                        o = PV[:, 0:4 * (DH + 1)].rearrange("p (i d) -> p i d", d=DH + 1)
                        v.reciprocal(rs[:, u % 2, :].unsqueeze(2), o[:, :, DH:DH + 1]).then_inc(S["rs_done"], 1)
                        dve.wait_ge(S["rs_done"], u + 1)
                        if u >= 2:
                            dve.wait_ge(S["ot_done"], u - 1)
                        v.tensor_tensor(ON[:, u % 2, :].rearrange("p (i d) -> p i d", d=DH), o[:, :, 0:DH],
                                        rs[:, u % 2, :].unsqueeze(2).to_broadcast([128, 4, DH]), ALU.mult)\
                            .then_inc(S["on_done"], 1)

                    for a in range(2):
                        J, U = K0[a], U0 * a
                        layer_norm(a, (xin, xres)[a])
                        input_lo(a)

                        def v_take(p):
                            ps = take(("v", a, p))
                            v.tensor_copy(v_sb[0:J, p % 2, :, :, 0:DH],
                                          ps[0:J, :].rearrange("p (b h d) -> p b h d", b=GB, h=2)).then_inc(S["v_done"], 1)

                        v_take(0)
                        for s in range(U0 + 4):
                            if s < U0:
                                _, sub = softmax_in(U + s, 4, J, J)
                                sub.then_inc(S["sub_done"], 1)
                            if 0 <= s - 2 < U0:
                                unit_out(U + s - 2)
                            if s < U0 and s % 2 == 1 and s // 2 + 1 < NP:
                                v_take(s // 2 + 1)
                            if 0 <= s - 4 < U0:
                                u, half = U + s - 4, s % 2
                                dve.wait_ge(S["wo_done"], u + 1)
                                dve.wait_ge(S["bias_added"], a + 1)
                                if u % U0 >= 2:
                                    dve.wait_ge(S["x_done"], u - 1)
                                xb = xres[:, 2 * half:2 * half + 2, :]
                                v.tensor_tensor(xb, PW[:, 0:2 * C].rearrange("p (b c) -> p b c", c=C), xb, ALU.add)\
                                    .then_inc(S["x_done"], 1)
                        dve.wait_ge(S["x_done"], U + U0)

                    layer_norm(2, xres)
                    input_lo(2)
                    for t in range(FF // 128):
                        ps = take(("up", t))
                        dve.wait_ge(S["gelu_done"], t + 1)
                        v.scalar_tensor_tensor(hT[:, t, :], ps[:, :], b_1[:, t:t + 1], gl[:, t % 2, :],
                                               ALU.add, ALU.mult).then_inc(S["h_done"], 1)
                    for b in range(GB):
                        ps = take(("down", b))
                        dve.wait_ge(S["bias_added"], 3)
                        v.tensor_tensor(xres[:, b, :], ps[:, 0:C], xres[:, b, :], ALU.add).then_inc(S["down_added"], 1)
                    dve.wait_ge(S["down_added"], GB)

                    last = None
                    for b in range(GB):
                        v.tensor_copy(nx[:, b, 0:128], xres[:, b, 0:128]).then_inc(S["nx_done"], 1)
                        v.tensor_copy(nx[:, b, 128:256].rearrange("p (r m) -> p r m", m=M),
                                      xres[:, b, 128:C].unsqueeze(1).to_broadcast([128, 4, M])).then_inc(S["nx_done"], 1)
                    input_lo(3)
                    for r in range(2):
                        ps = take(("k1", r))
                        r0 = 96 * r
                        for b in range(GB):
                            text = ps[r0:128, TS * b:TS * b + TT].unsqueeze(1).to_broadcast([128 - r0, 4, TT])
                            own = head_of_row[r0:128, :].unsqueeze(2).to_broadcast([128 - r0, 4, TT])
                            v.tensor_tensor(kbd[r0:128, r, b, :, 0:TT], text, own, ALU.mult)
                            ipk = ps[r0:128, GB * TS + NIP * b:GB * TS + NIP * b + NIP].unsqueeze(1)\
                                .to_broadcast([128 - r0, 4, NIP])
                            own = head_of_row[r0:128, :].unsqueeze(2).to_broadcast([128 - r0, 4, NIP])
                            last = v.tensor_tensor(kbd[r0:128, r, b, :, TT:T], ipk, own, ALU.mult)
                        last.then_inc(S["kbd_done"], 1)
                    ps = take(("vip", 0))
                    v.tensor_copy(vip_sb[:, :], ps[0:GB * NIP, 0:C]).then_inc(S["vip_done"], 1)

                    def l1_context(b):
                        ps = take(("gram", b))
                        if b >= 2:
                            dve.wait_ge(S["pv_done"], 2 * U0 + W1 * (b - 1))
                        v.tensor_copy(gv[:, b % 2, :, D1:D1 + TT], ps[0:TT, 0:TT].unsqueeze(1).to_broadcast([TT, NP, TT]))
                        v.tensor_copy(gv[:, b % 2, :, D1 + TT:D1 + T],
                                      ps[0:TT, T:T + NIP].unsqueeze(1).to_broadcast([TT, NP, NIP])).then_inc(S["gram_done"], 1)
                        ps = take(("v1", b))
                        blk = gv[:, b % 2, :, :]
                        for h in range(2):
                            last = v.tensor_copy(blk[:, :, (D1 + GS) * h:(D1 + GS) * h + D1],
                                                 ps[0:TT, 0:C].rearrange("p (q h d) -> p q h d", h=2, d=D1)[:, :, h, :])
                        last.then_inc(S["gv_done"], 1)
                        ps = take(("vbd", b))
                        v.tensor_tensor(vbd_sb[:, b % 2, :, :], ps[0:H * NIP, 0:C].rearrange("p (h d) -> p h d", d=D1),
                                        own_head[:, :, :], ALU.mult).then_inc(S["vbd_done"], 1)

                    def l1_unit_out(u, b, w):
                        dve.wait_ge(S["pv_done"], u + 1)
                        o = PV[:, 0:4 * GV].rearrange("p (i d) -> p i d", d=GV)
                        hs = slice(4 * w, 4 * w + 4)
                        v.reciprocal(rr[:, b % 2, hs].unsqueeze(2), o[:, :, D1 + T:D1 + T + 1]).then_inc(S["rs_done"], 1)
                        dve.wait_ge(S["rs_done"], u + 1)
                        r = rr[:, b % 2, hs]
                        for i in range(4):
                            c0 = GV * i + (D1 + GS) * (i % 2)
                            v.tensor_scalar(o1[:, b % 2, 4 * w + i, :], PV[:, c0:c0 + D1], r[:, i:i + 1], None, ALU.mult)
                        v.tensor_tensor(sem4[:, b % 2, hs, :], o[:, :, D1 + TT:D1 + T],
                                        r.unsqueeze(2).to_broadcast([128, 4, NIP]), ALU.mult)
                        pr = SE[:, u % 3, 0:4 * TT].rearrange("p (i j) -> p i j", j=TT)
                        v.tensor_tensor(gp, o[:, :, D1:D1 + TT], pr, ALU.mult).then_inc(S["gp_done"], 1)
                        dve.wait_ge(S["gp_done"], u - 2 * U0 + 1)
                        v.tensor_reduce(qq[:, b % 2, hs], gp, AX, ALU.add).then_inc(S["on_done"], 1)

                    def l1_tail_a(b):
                        k = b % 2
                        dve.wait_ge(S["n20_done"], b + 1)
                        then(v.tensor_tensor(r20[:, 1, :], r20[:, 0, :], rr[:, k, :], ALU.mult))
                        then(v.tensor_scalar(r20[:, 2, :], r20[:, 1, :], EPS_L2, None, ALU.max))
                        then(v.reciprocal(r20[:, 3, :], r20[:, 2, :]))
                        then(v.scalar_tensor_tensor(sem4[:, k, :, :], sem4[:, k, :, :], SEM_SCALE,
                                                    r20[:, 3, :].unsqueeze(2).to_broadcast([128, H, NIP]), ALU.mult, ALU.mult))
                        then(v.scalar_tensor_tensor(sip[:, k, :, :], sip[:, k, :, :], SCALE1, sem4[:, k, :, :],
                                                    ALU.mult, ALU.add))
                        then(v.tensor_reduce(r20[:, 1, :], sip[:, k, :, :], AX, ALU.max))
                        v.tensor_tensor(sip[:, k, :, :], sip[:, k, :, :],
                                        r20[:, 1, :].unsqueeze(2).to_broadcast([128, H, NIP]), ALU.subtract)\
                            .then_inc(S["sip_done"], 1)

                    def l1_tail_b(b):
                        k = b % 2
                        dve.wait_ge(S["sipe_done"], b + 1)
                        then(v.tensor_reduce(r20[:, 2, :], sip[:, k, :, :], AX, ALU.add))
                        then(v.reciprocal(r20[:, 3, :], r20[:, 2, :]))
                        then(v.tensor_scalar(r20[:, 2, :], r20[:, 3, :], fside[:, 0:1], None, ALU.mult))
                        v.tensor_tensor(sip[:, k, :, :], sip[:, k, :, :],
                                        r20[:, 2, :].unsqueeze(2).to_broadcast([128, H, NIP]), ALU.mult)\
                            .then_inc(S["mask_done"], 1)

                    def l1_tail_c(b):
                        k = b % 2
                        ps = take(("ip", b))
                        if b:
                            dve.wait_ge(S["job_full"], JOB[("oT1", b - 1)] + 1)
                        v.tensor_tensor(o1b, ps[:, 0:C], o1[:, k, :, :].rearrange("p h d -> p (h d)"), ALU.add)\
                            .then_inc(S["o1_done"], 1)
                        ps = take(("y", b))
                        v.tensor_tensor(yo[:, b, :], ps[:, 0:C], xres[:, b, :], ALU.add).then_inc(S["y_done"], 1)

                    UB = 2 * U0
                    dve.wait_ge(S["bias_added"], 4)
                    for s in range(U1 + 2):
                        if s < U1:
                            b, w = s // W1, s % W1
                            if w == 0:
                                l1_context(b)
                            sc, sub = softmax_in(UB + s, 4, TT, T)
                            ips = PS[s % 2][:, 0:4 * T].rearrange("p (i j) -> p i j", j=T)[:, :, TT:T]
                            v.tensor_copy(sip[:, b % 2, 4 * w:4 * w + 4, :], ips).then_inc(S["sub_done"], 1)
                        if 0 <= s - 2 < U1:
                            b, w = (s - 2) // W1, (s - 2) % W1
                            l1_unit_out(UB + s - 2, b, w)
                            if b >= 1 and w == 1:
                                l1_tail_a(b - 1)
                            if b >= 1 and w == 2:
                                l1_tail_b(b - 1)
                                l1_tail_c(b - 1)
                    l1_tail_a(GB - 1)
                    l1_tail_b(GB - 1)
                    l1_tail_c(GB - 1)

                @block.gpsimd
                def _(pool):
                    g = nc.gpsimd
                    for h in range(2):
                        g.memset(qk[DH:128, 3 * h + 1, :], 0.0).then_inc(S["k_zero"], 1)
                        pool.wait_ge(S["k_zero"], 2 * h + 1)
                        g.memset(qk[0:DH, 3 * h + 2, :], 0.0).then_inc(S["k_zero"], 1)
                        pool.wait_ge(S["k_zero"], 2 * h + 2)
                    pool.wait_ge(S["c_sq"], GB)
                    g.tensor_tensor(cst[:, 1, :], cst[:, 0, :], p_half[0:TS, 0:GB], ALU.pow).then_inc(S["pool_c"], 1)
                    steps = [1]
                    for k in range(3):
                        pool.wait_ge(S["ln_stats"], k + 1)
                        g.tensor_scalar(vp[:, :].unsqueeze(2), mv[:, :, 1:2], EPS_LN, None, ALU.add).then_inc(S["pool_c"], 1)
                        steps[0] += 1
                        pool.wait_ge(S["pool_c"], steps[0])
                        g.tensor_tensor(rstd[:, :], vp[:, :], p_mhalf[:, :], ALU.pow).then_inc(S["rstd_done"], 1)
                        pool.wait_ge(S["ln_t"], k + 1)
                        g.tensor_tensor(xres[:, :, :], (xin, xres, xres)[k][:, :, :],
                                        bias[:, k, :].unsqueeze(1).to_broadcast([128, GB, C]), ALU.add)\
                            .then_inc(S["bias_added"], 1)
                    pool.wait_ge(S["nx_done"], 2 * GB * 4)
                    g.tensor_tensor(xres[:, :, :], xres[:, :, :],
                                    bias[:, 3, :].unsqueeze(1).to_broadcast([128, GB, C]), ALU.add)\
                        .then_inc(S["bias_added"], 1)
                    for b in range(GB):
                        pool.wait_ge(S["on_done"], 2 * U0 + W1 * (b + 1))
                        g.tensor_tensor(r20[:, 0, :], qq[:, b % 2, :], p_half[:, :], ALU.pow).then_inc(S["n20_done"], 1)

            nc.sync.sem_clear(range(nums[0], nums[-1] + 1))
            nc.all_engine_barrier()


_INS = ['x', 'ctx_2048', 'fside_S_0',
        'L0_xattn_a1_wq', 'L0_xattn_a1_wk', 'L0_xattn_a1_wv', 'L0_xattn_a1_wo', 'L0_xattn_a1_bo',
        'L0_xattn_a2_wq', 'L0_xattn_a2_wk', 'L0_xattn_a2_wv', 'L0_xattn_a2_wo', 'L0_xattn_a2_bo',
        'L0_xattn_ff_w1', 'L0_xattn_ff_b1', 'L0_xattn_ff_w2', 'L0_xattn_ff_b2',
        'L0_xattn_ln1_g', 'L0_xattn_ln1_b', 'L0_xattn_ln2_g', 'L0_xattn_ln2_b', 'L0_xattn_ln3_g', 'L0_xattn_ln3_b',
        'L1_xattn_W_q', 'L1_xattn_W_k', 'L1_xattn_W_v', 'L1_xattn_W_k_ip', 'L1_xattn_W_v_ip', 'L1_xattn_W_out',
        'L1_xattn_b_out']


def kernel(**inputs):
    import numpy as _np
    import concourse.bacc as _bacc
    from concourse import mybir as _mybir
    from concourse.bass_utils import run_bass_kernel_spmd as _run

    nc = _bacc.Bacc("TRN2", target_bir_lowering=False, num_devices=1, dynamic_dma_scratch_size=1024)
    arrays, aps = {}, {}
    for name in _INS:
        a = _np.ascontiguousarray(inputs[name])
        arrays[f"in_{name}_dram"] = a
        aps[name] = nc.dram_tensor(f"in_{name}_dram", a.shape, _mybir.dt.from_np(a.dtype), kind="ExternalInput").ap()
    out = nc.dram_tensor("out_dram", inputs["x"].shape, _mybir.dt.float32, kind="ExternalOutput").ap()
    xattn_program(nc, aps, out)
    r = _run(nc, [arrays], core_ids=[0])
    return r.results[0]["out_dram"]
```

```python
import concourse.bass as bass
from concourse import mybir
from contextlib import ExitStack



def xattn_program(nc: bass.Bass, D, out: bass.AP):
    fp32 = mybir.dt.float32
    f32r = mybir.dt.float32r
    ALU = mybir.AluOpType
    ACT = mybir.ActivationFunctionType
    AX = mybir.AxisListType.X

    x_dram, ctx_dram = D["x"], D["ctx_2048"]
    B, N, C = x_dram.shape
    T, E = ctx_dram.shape[1:]
    H, DH = 20, 64
    INNER = H * DH
    FF = 4 * C
    GB = 4
    GROUPS = B // GB
    NP = H // 2
    HB = GB // 2
    HT = HB * 128
    U0 = NP * 2
    M = C - 128
    NIP = 4
    TT = T - NIP
    TS = T + NIP + 1
    D1 = C // H
    GS = TT + NIP + 1
    GV = GS + 2 * D1
    W1 = 5
    U1 = GB * W1
    SCALE0, SCALE1 = DH ** -0.5, D1 ** -0.5
    SEM_SCALE, EPS_LN, EPS_L2 = 0.5, 1e-5, 1e-12
    K0 = [N, T]
    NL0 = 2 * U0
    F = FF // 128

    GAP = 10
    FIRST, LAST = -4, 83

    def unit_at(s):
        if 0 <= s < NL0:
            return s
        return s - GAP if NL0 + GAP <= s < NL0 + GAP + U1 else None

    def l0_unit(s):
        n = unit_at(s)
        return n if n is not None and n < NL0 else None

    def l1_unit(s):
        n = unit_at(s)
        return n if n is not None and n >= NL0 else None

    NORM_SLOT = {(0, 0): FIRST, (0, 1): 2, (1, 0): 16, (1, 1): 26, (2, 0): 36, (3, 0): 45, (2, 1): 46, (3, 1): 50}
    NORMS = list(NORM_SLOT)
    REAL_NORMS = [kh for kh in NORMS if kh[0] < 3]

    def norms_at(s):
        return [kh for kh in NORMS if NORM_SLOT[kh] == s]

    FF_SLOT = [40 + t for t in range(F)] + [48, 48, 48, 49, 49]
    DOWN_SLOT = [45, 50]
    Q1_SLOT = [47, 52]
    K1_SLOT = [43, 51]
    CTX1_SLOT = [41, 42, 57, 62]
    TAIL_SLOT = [NL0 + GAP + W1 * (b + 2) for b in range(GB)]

    def early_jobs(s):
        jobs = [("xT",) + kh for kh in norms_at(s - 1)]
        for b in range(GB):
            for d, kind in ((2, "ipT"), (3, "ip"), (4, "oT1"), (5, "y")):
                if s == TAIL_SLOT[b] + d:
                    jobs.append((kind, b))
        return jobs

    def mid_jobs(s):
        n = l0_unit(s + 2)
        return [("qk", n)] if n is not None else []

    def late_jobs(s):
        n = l0_unit(s - 1)
        jobs = [("v", n // 2)] if n is not None and n % 2 == 0 else []
        if s == FIRST + 1:
            jobs += [("cT", 0), ("cT", 1)]
        jobs += [("ff", i) for i in range(2 * F) if FF_SLOT[i] == s]
        for h in range(2):
            if s == DOWN_SLOT[h]:
                jobs.append(("down", h))
            if s == Q1_SLOT[h]:
                jobs.append(("q1", h))
            if s == K1_SLOT[h]:
                jobs.append(("k1", h))
        if s == FF_SLOT[0]:
            jobs.append(("vip", 0))
        jobs += [("ctx1", b) for b in range(GB) if CTX1_SLOT[b] == s]
        return jobs

    JOBS = [j for s in range(FIRST, LAST) for j in early_jobs(s) + mid_jobs(s) + late_jobs(s)]
    JOB = {name: n for n, name in enumerate(JOBS)}

    def read_out(name):
        kind, i = name[0], name[-1]
        if kind == "xT":
            return [("nT_dve", NORMS.index(name[1:]) + 1)]
        if kind == "qk":
            return [("qk_act", i + 1), ("qk_dve", i + 1)]
        if kind == "ctx1":
            return [("gram_done", i + 1), ("gv_done", i + 1)]
        return [({"v": "v_done", "cT": "cT_dve", "ff": "h_done", "down": "down_added", "q1": "q1_done",
                  "k1": "kbd_done", "vip": "vip_done",
                  "ipT": "ipT_done", "ip": "o1_done", "oT1": "o1T_done", "y": "y_done"}[kind], i + 1)]


    ctx = ExitStack()
    with ctx:
        def sb(name, shape, dt=fp32):
            return ctx.enter_context(nc.sbuf_tensor(name, shape, dt))

        def split_weights(name, n):
            return (sb(name + "_hi", [128, n], f32r), sb(name + "_lo", [128, n], f32r),
                    sb(name + "_rem", [128, n], f32r))

        w_q = [split_weights("w_q0", INNER), split_weights("w_q1", INNER)]
        w_k0 = split_weights("w_k0", INNER)
        w_v0 = split_weights("w_v0", INNER)
        w_kc = sb("w_kc", [128, 2, 2, INNER], f32r)
        w_vc = sb("w_vc", [128, 2, 2, INNER], f32r)
        w_o = [sb("w_o0", [128, NP, C]), sb("w_o1", [128, NP, C])]
        w_1 = split_weights("w_1", 2 * FF)
        w_2 = sb("w_2", [128, FF // 128, C])
        w_q1 = split_weights("w_q1h", C)
        w_k1 = sb("w_k1h", [128, 2, 2, C], f32r)
        w_v1 = sb("w_v1h", [128, 2, 2, C], f32r)
        w_kip = sb("w_kip", [128, 2, C])
        w_vip = sb("w_vip", [128, 2, C])
        w_out = sb("w_out", [128, C])
        w_out_rem = sb("w_out_rem", [128, C])
        ln_g = sb("ln_g", [128, 3, C])
        ln_b = sb("ln_b", [128, 3, C])
        bias = sb("bias", [128, 4, C])
        b_1 = sb("b_1", [128, 2 * FF // 128])
        fside = sb("fside", [128, 1])
        ident = sb("ident", [128, 128])
        is_ip = sb("is_ip", [TS, 1])
        not_ip = sb("not_ip", [TS, 1])
        head_of_row = sb("head_of_row", [128, 4])
        own_head = sb("own_head", [H * NIP, H, D1])
        pick = sb("pick", [GB * NIP, GB, H * NIP])
        p_half = sb("p_half", [128, H])
        p_mhalf = sb("p_mhalf", [128, GB])
        xin = sb("xin", [128, GB, C])
        xres = sb("xres", [128, GB, C])
        cin = sb("cin", [TS, GB, E])
        cT = sb("cT", [128, 2, 2, GB * TS], f32r)
        cipT = sb("cipT", [128, 2, GB * NIP])
        cst = sb("cst", [TS, 4, GB])
        lt = sb("lt", [128, HB, C])
        nx = sb("nx", [128, HB, 256])
        nT = sb("nT", [128, 2, 3, HT], f32r)
        st6 = sb("st6", [128, HB, 6])
        mv = sb("mv", [128, HB, 2])
        rstd = sb("rstd", [128, HB])
        vp = sb("vp", [128, HB])
        qk = sb("qk", [128, 2, 3, HT])
        v_sb = sb("v_sb", [128, 2, HB, 4, DH + 1])
        SE = sb("SE", [128, 3, 512])
        PTs = sb("PTs", [128, 2, 512])
        work = sb("work", [128, 1024])
        ON = work[:, 0:512].rearrange("p (i n) -> p i n", i=2)
        OTs = work[:, 512:1024].rearrange("p (i n) -> p i n", i=2)
        WOs = sb("WOs", [128, 2, HB, C])
        mx = sb("mx", [128, 2, 4])
        rs = sb("rs", [128, 2, 4])
        hT = sb("hT", [128, F, HT])
        q1T = sb("q1T", [128, 2, 2, HT])
        vip_sb = sb("vip_sb", [GB * NIP, C])
        vbd_sb = sb("vbd_sb", [H * NIP, GB, H, D1])
        gv = sb("gv", [TT, 2, NP, GV])
        sip = sb("sip", [128, 3, H, NIP])
        qq = sb("qq", [128, 2, H])
        rr = sb("rr", [128, 2, H])
        r20 = sb("r20", [128, 4, H])
        o1 = sb("o1", [128, 2, H, D1])
        own16 = r20[:, 0, 0:16]
        gl = xin[:, :, :].rearrange("p b c -> p (b c)")[:, 0:2 * HT].rearrange("p (i n) -> p i n", i=2)
        SE_flat = SE[:, :, :].rearrange("p i n -> p (i n)")
        SE1 = SE_flat[:, 0:5 * 4 * TT].rearrange("p (i n) -> p i n", i=5)
        csq = WOs[0:TS, 0, :, :].rearrange("p b c -> p (b c)")[:, 0:E]
        kbd = [t[:, 0:2 * HB * 4 * T].rearrange("p (r b h t) -> p r b h t", r=2, b=HB, h=4)
               for t in (qk[:, :, :, :].rearrange("p a i n -> p (a i n)"), hT[:, :, :].rearrange("p a n -> p (a n)"))]
        GP = 4 * TT
        gs = [work[:, GP * i:GP * i + GP].rearrange("p (i t) -> p i t", i=4) for i in range(2)]
        o1T = work[:, 584:840]
        sem4 = work[:, 840:1000].rearrange("p (k h n) -> p k h n", k=2, h=H)
        WOs_flat = WOs[:, :, :, :].rearrange("p a b c -> p (a b c)")
        o1b = WOs_flat[:, 0:C]
        ipTs = WOs_flat[0:H * NIP, C:C + 128]

        PG = [ctx.enter_context(nc.psum_tensor(f"PG{i}", [128, 512], fp32)) for i in range(2)]
        PS = [ctx.enter_context(nc.psum_tensor(f"PS{i}", [128, 512], fp32)) for i in range(2)]
        PT = ctx.enter_context(nc.psum_tensor("PT", [128, 512], fp32))
        PV = ctx.enter_context(nc.psum_tensor("PV", [128, 512], fp32))
        PO = ctx.enter_context(nc.psum_tensor("PO", [128, 512], fp32))
        PW = ctx.enter_context(nc.psum_tensor("PW", [128, 512], fp32))

        def pv_bank(n):
            return PO if n >= NL0 and n % 2 else PV

        def pt_bank(n):
            return PW if n >= NL0 and n % 2 else PT

        def sem(name):
            return ctx.enter_context(nc.semaphore(name))

        stage_in = [sem("stage_in0"), sem("stage_in1")]
        stage_used = sem("stage_used")
        plain_in = sem("plain_in")
        setup_dve = sem("setup_dve")
        setup_pool = sem("setup_pool")

        SPLITS = []
        for name, tiles in (("L0_xattn_a1_wq", w_q[0]), ("L0_xattn_a1_wk", w_k0), ("L0_xattn_a1_wv", w_v0),
                            ("L0_xattn_a2_wq", w_q[1]), ("L0_xattn_ff_w1", w_1), ("L1_xattn_W_q", w_q1)):
            n = D[name].shape[1]
            SPLITS.append(([(D[name][0:128, :], 0, 128)], tiles[0][:, :], tiles[1][:, :], n))
            SPLITS.append(([(D[name][128:C, :], M * r, M * r + M) for r in range(4)], tiles[2][:, :], None, n))
        for name, tile in (("L0_xattn_a2_wk", w_kc), ("L0_xattn_a2_wv", w_vc),
                           ("L1_xattn_W_k", w_k1), ("L1_xattn_W_v", w_v1)):
            n = D[name].shape[1]
            for c in range(2):
                SPLITS.append(([(D[name][128 * c:128 * c + 128, :], 0, 128)], tile[:, c, 0, :], tile[:, c, 1, :], n))
        stage = [hT[:, :, :].rearrange("p a b -> p (a b)"), qk[:, :, :, :].rearrange("p a i b -> p (a i b)")]

        PLAIN = []
        for a, w in enumerate(("L0_xattn_a1_wo", "L0_xattn_a2_wo")):
            PLAIN.append((w_o[a][:, :, :], D[w].rearrange("(p k) n -> k p n", k=128)))
        PLAIN.append((w_2[:, :, :], D["L0_xattn_ff_w2"].rearrange("(p k) n -> k p n", k=128)))
        for w, t in (("L1_xattn_W_k_ip", w_kip), ("L1_xattn_W_v_ip", w_vip)):
            PLAIN.append((t[:, :, :], D[w].rearrange("(c k) n -> k c n", k=128)))
        PLAIN.append((w_out[:, :], D["L1_xattn_W_out"][0:128, :]))
        PLAIN.append((w_out_rem[96:128, :], D["L1_xattn_W_out"][128:C, :]))
        for k in range(3):
            PLAIN.append((ln_g[:, k, :], D[f"L0_xattn_ln{k + 1}_g"].partition_broadcast(128)))
            PLAIN.append((ln_b[:, k, :], D[f"L0_xattn_ln{k + 1}_b"].partition_broadcast(128)))
        for k, w in enumerate(("L0_xattn_a1_bo", "L0_xattn_a2_bo", "L0_xattn_ff_b2", "L1_xattn_b_out")):
            PLAIN.append((bias[:, k, :], D[w].partition_broadcast(128)))
        PLAIN.append((b_1[:, :], D["L0_xattn_ff_b1"].rearrange("(t p) -> p t", p=128)))
        PLAIN.append((fside[:, :], D["fside_S_0"].rearrange("(p a) -> p a", a=1)))

        with nc.Block() as block:
            @block.sync
            def _(sp):
                count = [0, 0]
                for i, (parts, _, _, n) in enumerate(SPLITS):
                    if i >= 2:
                        sp.wait_ge(stage_used, i - 1)
                    for src, p0, p1 in parts:
                        sp.dma_start(stage[i % 2][p0:p1, 0:n], src).then_inc(stage_in[i % 2], 16)

            @block.scalar
            def _(act):
                for dst, src in PLAIN:
                    act.dma_start(dst, src, allow_slow_non_contiguous=True).then_inc(plain_in, 16)
                act.wait_ge(plain_in, 16 * len(PLAIN))

            @block.vector
            def _(dve):
                count = [0, 0]
                steps = 0
                for i, (parts, hi, lo, n) in enumerate(SPLITS):
                    count[i % 2] += 16 * len(parts)
                    dve.wait_ge(stage_in[i % 2], count[i % 2])
                    s = stage[i % 2]
                    nc.vector.tensor_copy(hi, s[:, 0:n]).then_inc(setup_dve, 1)
                    steps += 1
                    dve.wait_ge(setup_dve, steps)
                    if lo is not None:
                        nc.vector.tensor_tensor(lo, s[:, 0:n], hi.bitcast(fp32), ALU.subtract).then_inc(stage_used, 1)
                    else:
                        nc.vector.tensor_tensor(hi[M:2 * M], s[M:2 * M, 0:n], hi[M:2 * M].bitcast(fp32), ALU.subtract)
                        nc.vector.tensor_tensor(hi[3 * M:4 * M], s[3 * M:4 * M, 0:n], hi[3 * M:4 * M].bitcast(fp32),
                                                ALU.subtract).then_inc(stage_used, 1)
                dve.wait_ge(stage_used, len(SPLITS))
                nc.vector.memset(v_sb[:, :, :, :, :], 1.0)
                nc.vector.memset(gv[:, :, :, :], 1.0)

            @block.gpsimd
            def _(pool):
                g = nc.gpsimd
                steps = [0]

                def done(ins):
                    steps[0] += 1
                    ins.then_inc(setup_pool, 1)
                    pool.wait_ge(setup_pool, steps[0])

                g.memset(p_half[:, :], 0.5)
                g.memset(p_mhalf[:, :], -0.5)
                done(g.memset(cin[:, :, :], 0.0))
                done(g.memset(ident[:, :], 0.0))
                done(g.affine_select(out=ident[:, :], in_=ident[:, :], compare_op=ALU.not_equal, fill=1.0,
                                     base=0, pattern=[[-1, 128]], channel_multiplier=1))
                done(g.memset(is_ip[:, :], 1.0))
                done(g.affine_select(out=is_ip[:, :], in_=is_ip[:, :], compare_op=ALU.is_ge, fill=0.0,
                                     base=-T, pattern=[[0, 1]], channel_multiplier=1))
                done(g.tensor_scalar(not_ip[:, :], is_ip[:, :], -1.0, 1.0, ALU.mult, ALU.add))
                done(g.memset(own16, 1.0))
                done(g.affine_select(out=own16, in_=own16, compare_op=ALU.is_ge, fill=0.0,
                                     base=0, pattern=[[-D1, 16]], channel_multiplier=1))
                done(g.affine_select(out=own16, in_=own16, compare_op=ALU.is_ge, fill=0.0,
                                     base=D1 - 1, pattern=[[D1, 16]], channel_multiplier=-1))
                done(g.tensor_tensor(head_of_row[:, :], own16[:, 0:4], own16[:, 4:8], ALU.add))
                done(g.tensor_tensor(head_of_row[:, :], head_of_row[:, :], own16[:, 8:12], ALU.add))
                done(g.tensor_tensor(head_of_row[:, :], head_of_row[:, :], own16[:, 12:16], ALU.add))
                done(g.memset(own_head[:, :, :], 1.0))
                done(g.affine_select(out=own_head[:, :, :], in_=own_head[:, :, :], compare_op=ALU.is_ge, fill=0.0,
                                     base=0, pattern=[[-NIP, H], [0, D1]], channel_multiplier=1))
                done(g.affine_select(out=own_head[:, :, :], in_=own_head[:, :, :], compare_op=ALU.is_ge, fill=0.0,
                                     base=NIP - 1, pattern=[[NIP, H], [0, D1]], channel_multiplier=-1))
                pk = pick[:, :, :].rearrange("p b (h n) -> p b h n", n=NIP)
                done(g.memset(pick[:, :, :], 0.0))
                done(g.affine_select(out=pk, in_=pk, compare_op=ALU.not_equal, fill=1.0, base=0,
                                     pattern=[[-NIP, GB], [0, H], [-1, NIP]], channel_multiplier=1))

        names = ["x_in", "c_in", "out_done", "job_full",
                 "ln_stats", "ln_t", "rstd_done", "nx_done", "nT_act", "nT_dve", "k_zero", "bias_added",
                 "c_sq", "c_pow", "c_dve", "cT_act", "cT_dve",
                 "qk_act", "qk_dve", "v_done",
                 "s_done", "mx_done", "sub_done", "exp_done", "pt_done", "pts_done", "pv_done", "rs_done",
                 "on_done", "ot_done", "ots_done", "wo_done", "wos_done", "x_done",
                 "gelu_done", "h_done", "down_added",
                 "q1_done", "kbd_done", "vip_done", "gram_done", "gv_done",
                 "gs_done", "gp_done", "qq_done", "n20_done", "d_chain", "sip_done", "sipe_done", "mask_done",
                 "ipT_done", "o1_done", "o1T_done", "y_done", "pool_own"]
        S = {n: sem(n) for n in names}
        nums = sorted(x.num for x in S.values())
        assert nums == list(range(nums[0], nums[0] + len(nums)))

        def bank(name):
            return PG[JOB[name] % 2]

        with nc.Fori(0, GROUPS) as grp:
            with nc.Block() as block:
                xg = x_dram.rearrange("(g b) n c -> g n b c", b=GB)
                cg = ctx_dram.rearrange("(g b) t e -> g t b e", b=GB)
                og = out.rearrange("(g b) n c -> g b n c", b=GB)

                @block.sync
                def _(sp):
                    sp.dma_start(xin[:, :, :], xg[grp, :, :, :]).then_inc(S["x_in"], 16)
                    sp.dma_start(cin[0:T, :, :], cg[grp, :, :, :]).then_inc(S["c_in"], 16)
                    sp.dma_start(cin[T:T + NIP, :, :], cg[grp, TT:T, :, :]).then_inc(S["c_in"], 16)
                    for b in range(GB):
                        sp.wait_ge(S["y_done"], b + 1)
                        sp.dma_start(og[grp, b, :, :], xres[:, b, :]).then_inc(S["out_done"], 16)
                    sp.wait_ge(S["out_done"], 16 * GB)

                @block.tensor
                def _(pe):
                    mm = nc.tensor.matmul
                    tr = nc.tensor.transpose
                    SPLIT3 = [(0, 0), (0, 1), (1, 0)]

                    def rows160(ps, w, c0, h):
                        mm(ps, w[0][:, c0:c0 + 128], nT[:, h, 0, :], start=True, stop=False)
                        mm(ps, w[1][:, c0:c0 + 128], nT[:, h, 0, :], start=False, stop=False)
                        mm(ps, w[0][:, c0:c0 + 128], nT[:, h, 2, :], start=False, stop=False)
                        return mm(ps, w[2][:, c0:c0 + 128], nT[:, h, 1, :], start=False, stop=True)

                    def rows160_out(ps, w, c0, n, h, b):
                        t = slice(128 * b, 128 * b + 128)
                        mm(ps, nT[:, h, 0, t], w[0][:, c0:c0 + n], start=True, stop=False)
                        mm(ps, nT[:, h, 0, t], w[1][:, c0:c0 + n], start=False, stop=False)
                        mm(ps, nT[:, h, 2, t], w[0][:, c0:c0 + n], start=False, stop=False)
                        return mm(ps, nT[:, h, 1, t], w[2][:, c0:c0 + n], start=False, stop=True)

                    def ctx_cols(ps, w, c0, h):
                        for c in range(2):
                            for i, (hw, hc) in enumerate(SPLIT3):
                                last = mm(ps, w[:, c, hw, c0:c0 + 128], cT[:, c, hc, HB * TS * h:HB * TS * (h + 1)],
                                          start=(c == 0 and i == 0), stop=(c == 1 and i == 2))
                        return last

                    def ctx_rows(ps, w, c0, n, b, rows):
                        for c in range(2):
                            for i, (hw, hc) in enumerate(SPLIT3):
                                last = mm(ps, cT[:, c, hc, TS * b:TS * b + rows], w[:, c, hw, c0:c0 + n],
                                          start=(c == 0 and i == 0), stop=(c == 1 and i == 2))
                        return last

                    def job(name):
                        kind, i = name[0], name[-1]
                        if JOB[name] >= 2:
                            for which, count in read_out(JOBS[JOB[name] - 2]):
                                pe.wait_ge(S[which], count)
                        ps = bank(name)
                        if kind == "cT":
                            pe.wait_ge(S["c_dve"], GB)
                            for b in range(GB):
                                last = tr(ps[:, TS * b:TS * b + TS], cin[:, b, 128 * i:128 * i + 128], ident[0:TS, 0:TS])
                        elif kind == "xT":
                            pe.wait_ge(S["nx_done"], NORMS.index(name[1:]) + 1)
                            for part in range(2):
                                for b in range(HB):
                                    last = tr(ps[:, HT * part + 128 * b:HT * part + 128 * b + 128],
                                              nx[:, b, 128 * part:128 * part + 128], ident[:, :])
                        elif kind == "qk":
                            a, h, p = i // U0, i // NP % 2, i % NP
                            if p == 0:
                                wait_nT(a, h)
                                if a == 1:
                                    pe.wait_ge(S["cT_act"], 2)
                                    pe.wait_ge(S["cT_dve"], 2)
                            rows160(ps[:, 0:HT], w_q[a], 128 * p, h)
                            if a == 0:
                                last = rows160(ps[:, HT:2 * HT], w_k0, 128 * p, h)
                            else:
                                last = ctx_cols(ps[:, HT:HT + HB * TS], w_kc, 128 * p, h)
                        elif kind == "v":
                            a, h, p = 2 * i // U0, 2 * i // NP % 2, 2 * i % NP
                            for b in range(HB):
                                o = ps[0:K0[a], 256 * b:256 * b + 256]
                                if a == 0:
                                    last = rows160_out(o, w_v0, 128 * p, 256, h, b)
                                else:
                                    last = ctx_rows(o, w_vc, 128 * p, 256, HB * h + b, T)
                        elif kind == "ff":
                            h, t = i // F, i % F
                            if t == 0:
                                wait_nT(2, h)
                            rows160(ps[:, 0:HT], w_1, FF + 128 * t, h)
                            last = rows160(ps[:, HT:2 * HT], w_1, 128 * t, h)
                        elif kind == "down":
                            pe.wait_ge(S["h_done"], F * (i + 1))
                            for b in range(HB):
                                for t in range(F):
                                    last = mm(ps[:, C * b:C * b + C], hT[:, t, 128 * b:128 * b + 128], w_2[:, t, :],
                                              start=(t == 0), stop=(t == F - 1))
                        elif kind == "q1":
                            wait_nT(3, i)
                            for r in range(2):
                                last = rows160(ps[:, HT * r:HT * r + HT], w_q1, M * r, i)
                        elif kind == "k1":
                            kw, iw = HB * TS, HB * NIP
                            if i == 0:
                                pe.wait_ge(S["cT_dve"], 2)
                            for r in range(2):
                                c0 = (kw + iw) * r
                                ctx_cols(ps[:, c0:c0 + kw], w_k1, M * r, i)
                                for c in range(2):
                                    last = mm(ps[:, c0 + kw:c0 + kw + iw], w_kip[:, c, M * r:M * r + 128],
                                              cipT[:, c, iw * i:iw * i + iw], start=(c == 0), stop=(c == 1))
                        elif kind == "vip":
                            for c in range(2):
                                last = mm(ps[0:GB * NIP, 0:C], cipT[:, c, :], w_vip[:, c, :], start=(c == 0), stop=(c == 1))
                        elif kind == "ctx1":
                            for c in range(2):
                                for j, (h0, h1) in enumerate(SPLIT3):
                                    mm(ps[0:TT, 0:TS], cT[:, c, h0, TS * i:TS * i + TT], cT[:, c, h1, TS * i:TS * i + TS],
                                       start=(c == 0 and j == 0), stop=(c == 1 and j == 2))
                            ctx_rows(ps[0:TT, TS:TS + C], w_v1, 0, C, i, TT)
                            pe.wait_ge(S["vip_done"], 1)
                            last = mm(ps[0:H * NIP, TS + C:TS + 2 * C], pick[:, i, :], vip_sb[:, :], start=True, stop=True)
                        elif kind == "ipT":
                            pe.wait_ge(S["mask_done"], i + 1)
                            last = tr(ps[0:H * NIP, 0:128], sip[:, i % 3, :, :].rearrange("p h n -> p (h n)"), ident[:, :])
                        elif kind == "ip":
                            pe.wait_ge(S["ipT_done"], i + 1)
                            pe.wait_ge(S["gv_done"], i + 1)
                            last = mm(ps[:, 0:C], ipTs, vbd_sb[:, i, :, :].rearrange("p h d -> p (h d)"),
                                      start=True, stop=True)
                        elif kind == "oT1":
                            pe.wait_ge(S["o1_done"], i + 1)
                            tr(ps[:, 0:128], o1b[:, 0:128], ident[:, :])
                            last = tr(ps[:, 128:256], o1b[:, M:C], ident[:, :])
                        elif kind == "y":
                            pe.wait_ge(S["o1T_done"], i + 1)
                            mm(ps[:, 0:C], o1T[:, 0:128], w_out[:, :], start=True, stop=False)
                            last = mm(ps[:, 0:C], o1T[96:128, 128:256], w_out_rem[96:128, :], start=False, stop=True)
                        last.then_inc(S["job_full"], 1)

                    def wait_nT(k, h):
                        pe.wait_ge(S["nT_act"], NORMS.index((k, h)) + 1)
                        pe.wait_ge(S["nT_dve"], NORMS.index((k, h)) + 1)

                    def scores(n):
                        if n >= 2:
                            pe.wait_ge(S["sub_done"], n - 1)
                        ps = PS[n % 2]
                        if n < NL0:
                            J, kstep = (N, 128) if n < U0 else (T, TS)
                            pe.wait_ge(S["qk_act"], n + 1)
                            pe.wait_ge(S["qk_dve"], n + 1)
                            if n == 0:
                                pe.wait_ge(S["k_zero"], 4)
                            for i in range(4):
                                b, k = i // 2, qk[:, n % 2, 1 + i % 2, :]
                                last = mm(ps[:, J * i:J * i + J], qk[:, n % 2, 0, 128 * b:128 * b + 128],
                                          k[:, kstep * b:kstep * b + J], start=True, stop=True)
                        else:
                            b, w = (n - NL0) // W1, (n - NL0) % W1
                            h = b // HB
                            if w == 0 and b % HB == 0:
                                pe.wait_ge(S["q1_done"], h + 1)
                                pe.wait_ge(S["kbd_done"], h + 1)
                            r, row = (0, 32 * w) if w < 4 else (1, 96)
                            last = mm(ps[:, 0:4 * T], q1T[row:row + 32, h, r, 128 * (b % HB):128 * (b % HB) + 128],
                                      kbd[h][row:row + 32, r, b % HB, :, :].rearrange("p h t -> p (h t)"),
                                      start=True, stop=True)
                        last.then_inc(S["s_done"], 1)

                    def probs_transposed(n):
                        pe.wait_ge(S["exp_done"], n + 1)
                        if n >= 1:
                            pe.wait_ge(S["pts_done"], n if n <= NL0 else n - 1)
                        if n == NL0 + 1:
                            pe.wait_ge(S["wos_done"], NL0)
                        PT = pt_bank(n)
                        for i in range(4):
                            if n < NL0:
                                J = K0[n // U0]
                                last = tr(PT[0:J, 128 * i:128 * i + 128], SE[:, n % 3, J * i:J * i + J], ident[:, :])
                            else:
                                last = tr(PT[0:TT, 128 * i:128 * i + 128], SE1[:, n % 5, TT * i:TT * i + TT], ident[:, :])
                        last.then_inc(S["pt_done"], 1)

                    def probs_v(n):
                        pe.wait_ge(S["pts_done"], n + 1)
                        if n >= 1:
                            pe.wait_ge(S["on_done"], n if n <= NL0 else n - 1)
                        if n == NL0 + 1:
                            pe.wait_ge(S["ots_done"], NL0)
                        PV = pv_bank(n)
                        if n < NL0:
                            pe.wait_ge(S["v_done"], n // 2 + 1)
                            J = K0[n // U0]
                            for i in range(4):
                                last = mm(PV[:, (DH + 1) * i:(DH + 1) * (i + 1)],
                                          PTs[0:J, n % 2, 128 * i:128 * i + 128],
                                          v_sb[0:J, n // 2 % 2, i // 2, 2 * (n % 2) + i % 2, :], start=True, stop=True)
                        else:
                            b, w = (n - NL0) // W1, (n - NL0) % W1
                            if n - NL0 >= 2:
                                pe.wait_ge(S["gs_done"], n - NL0 - 1)
                            pe.wait_ge(S["gv_done"], b + 1)
                            pe.wait_ge(S["gram_done"], b + 1)
                            for i in range(4):
                                off = D1 * (i % 2)
                                last = mm(PV[:, GV * i + off:GV * i + off + GS + D1],
                                          PTs[0:TT, n % 2, 128 * i:128 * i + 128],
                                          gv[:, b % 2, 2 * w + i // 2, off:off + GS + D1], start=True, stop=True)
                        last.then_inc(S["pv_done"], 1)

                    def out_transposed(n):
                        pe.wait_ge(S["on_done"], n + 1)
                        if n >= 1:
                            pe.wait_ge(S["ots_done"], n)
                        for b in range(HB):
                            last = tr(PO[:, 128 * b:128 * b + 128], ON[:, n % 2, 128 * b:128 * b + 128], ident[:, :])
                        last.then_inc(S["ot_done"], 1)

                    def out_projected(n):
                        pe.wait_ge(S["ots_done"], n + 1)
                        if n >= 1:
                            pe.wait_ge(S["wos_done"], n)
                        for b in range(HB):
                            last = mm(PW[:, C * b:C * b + C], OTs[:, n % 2, 128 * b:128 * b + 128],
                                      w_o[n // U0][:, n % NP, :], start=True, stop=True)
                        last.then_inc(S["wo_done"], 1)

                    for s in range(FIRST, LAST):
                        for name in early_jobs(s):
                            job(name)
                        if unit_at(s + 1) is not None:
                            scores(unit_at(s + 1))
                        if unit_at(s - 1) is not None:
                            probs_transposed(unit_at(s - 1))
                        if l0_unit(s - 4) is not None:
                            out_transposed(l0_unit(s - 4))
                        if l0_unit(s - 5) is not None:
                            out_projected(l0_unit(s - 5))
                        for name in mid_jobs(s):
                            job(name)
                        if unit_at(s - 2) is not None:
                            probs_v(unit_at(s - 2))
                        for name in late_jobs(s):
                            job(name)

                @block.scalar
                def _(act):
                    a_ = nc.scalar.activation

                    def take(name):
                        act.wait_ge(S["job_full"], JOB[name] + 1)
                        return bank(name)

                    def job(name):
                        kind, i = name[0], name[-1]
                        if kind == "cT":
                            a_(cT[:, i, 0, :], take(name)[:, 0:GB * TS], ACT.Copy).then_inc(S["cT_act"], 1)
                        elif kind == "xT":
                            a_(nT[:, i, 0:2, :].rearrange("p r n -> p (r n)"), take(name)[:, :], ACT.Copy)\
                                .then_inc(S["nT_act"], 1)
                        elif kind == "qk":
                            ps, kw = take(name), HT if i < U0 else HB * TS
                            a_(qk[:, i % 2, 0, :], ps[:, 0:HT], ACT.Copy)
                            a_(qk[0:DH, i % 2, 1, 0:kw], ps[0:DH, HT:HT + kw], ACT.Copy).then_inc(S["qk_act"], 1)
                        elif kind == "ff":
                            h, t = i // F, i % F
                            ps = take(name)
                            if i >= 2:
                                act.wait_ge(S["h_done"], i - 1)
                            a_(gl[:, i % 2, :], ps[:, 0:HT], ACT.Gelu, bias=b_1[:, F + t:F + t + 1])\
                                .then_inc(S["gelu_done"], 1)
                        elif kind == "q1":
                            a_(q1T[:, i, :, :].rearrange("p r n -> p (r n)"), take(name)[:, :], ACT.Copy)\
                                .then_inc(S["q1_done"], 1)
                        elif kind == "ctx1":
                            ps = take(name)
                            if i >= 2:
                                act.wait_ge(S["pv_done"], NL0 + W1 * (i - 1))
                            a_(gv[:, i % 2, :, D1:D1 + TT], ps[0:TT, 0:TT].unsqueeze(1).to_broadcast([TT, NP, TT]), ACT.Copy)
                            a_(gv[:, i % 2, :, D1 + TT:D1 + T],
                               ps[0:TT, T:T + NIP].unsqueeze(1).to_broadcast([TT, NP, NIP]), ACT.Copy)\
                                .then_inc(S["gram_done"], 1)
                        elif kind == "ipT":
                            a_(ipTs, take(name)[0:H * NIP, 0:128], ACT.Copy).then_inc(S["ipT_done"], 1)
                        elif kind == "oT1":
                            a_(o1T, take(name)[:, 0:256], ACT.Copy).then_inc(S["o1T_done"], 1)

                    def wo_out(n):
                        act.wait_ge(S["wo_done"], n + 1)
                        if n >= 2:
                            act.wait_ge(S["x_done"], n - 1)
                        a_(WOs[:, n % 2, :, :].rearrange("p b c -> p (b c)"), PW[:, 0:HB * C], ACT.Copy)\
                            .then_inc(S["wos_done"], 1)

                    def pt_out(n):
                        act.wait_ge(S["pt_done"], n + 1)
                        if n >= 2:
                            act.wait_ge(S["pv_done"], n - 1)
                        J = K0[n // U0] if n < NL0 else TT
                        a_(PTs[0:J, n % 2, :], pt_bank(n)[0:J, :], ACT.Copy).then_inc(S["pts_done"], 1)

                    def ot_out(n):
                        act.wait_ge(S["ot_done"], n + 1)
                        if n >= 2:
                            act.wait_ge(S["wo_done"], n - 1)
                        a_(OTs[:, n % 2, :], PO[:, 0:HT], ACT.Copy).then_inc(S["ots_done"], 1)

                    def exp(n):
                        act.wait_ge(S["sub_done"], n + 1)
                        if n < NL0:
                            e, scale = SE[:, n % 3, 0:4 * K0[n // U0]], SCALE0
                        else:
                            e, scale = SE1[:, n % 5, :], SCALE1
                        a_(e, e, ACT.Exp, scale=scale).then_inc(S["exp_done"], 1)

                    def gram_out(n):
                        act.wait_ge(S["pv_done"], n + 1)
                        act.wait_ge(S["on_done"], n + 1)
                        if n - NL0 >= 2:
                            act.wait_ge(S["qq_done"], n - NL0 - 1)
                        g = pv_bank(n)[:, 0:4 * GV].rearrange("p (i d) -> p i d", d=GV)[:, :, D1:D1 + TT]
                        a_(gs[n % 2], g, ACT.Copy).then_inc(S["gs_done"], 1)

                    for s in range(FIRST, LAST):
                        if s == FIRST:
                            act.wait_ge(S["c_in"], 32)
                            for b in range(GB):
                                if b:
                                    act.wait_ge(S["c_sq"], b)
                                a_(csq, cin[:, b, :], ACT.Square, accum_out=cst[:, 0, b:b + 1]).then_inc(S["c_sq"], 1)
                        for name in early_jobs(s):
                            job(name)
                        if l0_unit(s - 6) is not None:
                            wo_out(l0_unit(s - 6))
                        if l1_unit(s - 3) is not None:
                            gram_out(l1_unit(s - 3))
                        if unit_at(s - 1) is not None:
                            pt_out(unit_at(s - 1))
                        for name in mid_jobs(s):
                            job(name)
                        if l0_unit(s - 4) is not None:
                            ot_out(l0_unit(s - 4))
                        if unit_at(s) is not None:
                            exp(unit_at(s))
                        for b in range(GB):
                            if s == TAIL_SLOT[b]:
                                act.wait_ge(S["sip_done"], b + 1)
                                e = sip[:, b % 3, :, :]
                                a_(e, e, ACT.Exp).then_inc(S["sipe_done"], 1)
                        for name in late_jobs(s):
                            job(name)

                @block.vector
                def _(dve):
                    v = nc.vector
                    chain = [0]

                    def then(ins):
                        chain[0] += 1
                        ins.then_inc(S["d_chain"], 1)
                        dve.wait_ge(S["d_chain"], chain[0])

                    def take(name):
                        dve.wait_ge(S["job_full"], JOB[name] + 1)
                        return bank(name)

                    def norm_stats(k, h):
                        if k == 0:
                            dve.wait_ge(S["x_in"], 16)
                        else:
                            dve.wait_ge(S["x_done"], U0 * (k - 1) + NP * (h + 1))
                        x = (xin if k == 0 else xres)[:, HB * h:HB * h + HB, :]
                        for b in range(HB):
                            last = v.bn_stats(st6[:, b, :], x[:, b, :])
                        then(last)
                        for b in range(HB):
                            last = v.bn_aggr(mv[:, b, :], st6[:, b, :])
                        last.then_inc(S["ln_stats"], 1)

                    def norm_out(k, h):
                        i = REAL_NORMS.index((k, h)) + 1
                        x = (xin if k == 0 else xres)[:, HB * h:HB * h + HB, :]
                        dve.wait_ge(S["ln_stats"], i)
                        for b in range(HB):
                            last = v.scalar_tensor_tensor(lt[:, b, :], x[:, b, :], mv[:, b, 0:1], ln_g[:, k, :],
                                                          ALU.subtract, ALU.mult)
                        last.then_inc(S["ln_t"], 1)
                        dve.wait_ge(S["ln_t"], i)
                        dve.wait_ge(S["rstd_done"], i)
                        rest = lambda ap: ap[:, 128:C].unsqueeze(1).to_broadcast([128, 4, M])
                        for b in range(HB):
                            v.scalar_tensor_tensor(nx[:, b, 0:128], lt[:, b, 0:128], rstd[:, b:b + 1], ln_b[:, k, 0:128],
                                                   ALU.mult, ALU.add)
                            last = v.scalar_tensor_tensor(nx[:, b, 128:256].rearrange("p (r m) -> p r m", m=M),
                                                          rest(lt[:, b, :]), rstd[:, b:b + 1], rest(ln_b[:, k, :]),
                                                          ALU.mult, ALU.add)
                        last.then_inc(S["nx_done"], 1)

                    def l1_input(h):
                        dve.wait_ge(S["down_added"], h + 1)
                        x = xres[:, HB * h:HB * h + HB, :]
                        v.tensor_copy(nx[:, :, 0:128], x[:, :, 0:128])
                        for b in range(HB):
                            last = v.tensor_copy(nx[:, b, 128:256].rearrange("p (r m) -> p r m", m=M),
                                                 x[:, b, 128:C].unsqueeze(1).to_broadcast([128, 4, M]))
                        last.then_inc(S["nx_done"], 1)

                    def context_scale():
                        dve.wait_ge(S["c_pow"], 1)
                        then(v.tensor_scalar(cst[:, 2, :], cst[:, 1, :], EPS_L2, None, ALU.max))
                        then(v.reciprocal(cst[:, 3, :], cst[:, 2, :]))
                        then(v.tensor_scalar(cst[:, 2, :], cst[:, 3, :], is_ip[:, 0:1], not_ip[:, 0:1], ALU.mult, ALU.add))
                        for b in range(GB):
                            v.tensor_scalar(cin[:, b, :], cin[:, b, :], cst[:, 2, b:b + 1], None, ALU.mult)\
                                .then_inc(S["c_dve"], 1)

                    def job(name):
                        kind, i = name[0], name[-1]
                        if kind == "cT":
                            ps = take(name)
                            dve.wait_ge(S["cT_act"], i + 1)
                            v.tensor_tensor(cT[:, i, 1, :], ps[:, 0:GB * TS], cT[:, i, 0, :].bitcast(fp32), ALU.subtract)
                            ip = ps[:, 0:GB * TS].rearrange("p (b t) -> p b t", t=TS)[:, :, TT:T]
                            v.tensor_copy(cipT[:, i, :].rearrange("p (b n) -> p b n", n=NIP), ip)\
                                .then_inc(S["cT_dve"], 1)
                        elif kind == "xT":
                            ps = take(name)
                            dve.wait_ge(S["nT_act"], NORMS.index(name[1:]) + 1)
                            v.tensor_tensor(nT[:, i, 2, :], ps[:, 0:HT], nT[:, i, 0, :].bitcast(fp32), ALU.subtract)
                            v.tensor_tensor(nT[64:128, i, 1, :], ps[64:128, HT:2 * HT], nT[64:128, i, 1, :].bitcast(fp32),
                                            ALU.subtract).then_inc(S["nT_dve"], 1)
                        elif kind == "qk":
                            ps, kw = take(name), HT if i < U0 else HB * TS
                            dve.wait_ge(S["qk_act"], i + 1)
                            v.tensor_copy(qk[DH:128, i % 2, 2, 0:kw], ps[DH:128, HT:HT + kw]).then_inc(S["qk_dve"], 1)
                        elif kind == "v":
                            ps, J = take(name), K0[2 * i // U0]
                            v.tensor_copy(v_sb[0:J, i % 2, :, :, 0:DH],
                                          ps[0:J, :].rearrange("p (b h d) -> p b h d", b=HB, h=4)).then_inc(S["v_done"], 1)
                        elif kind == "ff":
                            h, t = i // F, i % F
                            ps = take(name)
                            dve.wait_ge(S["gelu_done"], i + 1)
                            v.scalar_tensor_tensor(hT[:, t, :], ps[:, HT:2 * HT], b_1[:, t:t + 1], gl[:, i % 2, :],
                                                   ALU.add, ALU.mult).then_inc(S["h_done"], 1)
                        elif kind == "down":
                            ps = take(name)
                            dve.wait_ge(S["bias_added"], NORMS.index((2, i)) + 1)
                            x = xres[:, HB * i:HB * i + HB, :]
                            v.tensor_tensor(x, ps[:, 0:HB * C].rearrange("p (b c) -> p b c", c=C), x, ALU.add)\
                                .then_inc(S["down_added"], 1)
                        elif kind == "k1":
                            ps, kw, iw = take(name), HB * TS, HB * NIP
                            for r in range(2):
                                r0, c0 = 96 * r, (kw + iw) * r
                                own = head_of_row[r0:128, :].unsqueeze(2)
                                for b in range(HB):
                                    text = ps[r0:128, c0 + TS * b:c0 + TS * b + TT].unsqueeze(1)
                                    image = ps[r0:128, c0 + kw + NIP * b:c0 + kw + NIP * b + NIP].unsqueeze(1)
                                    v.tensor_tensor(kbd[i][r0:128, r, b, :, 0:TT], text.to_broadcast([128 - r0, 4, TT]),
                                                    own.to_broadcast([128 - r0, 4, TT]), ALU.mult)
                                    last = v.tensor_tensor(kbd[i][r0:128, r, b, :, TT:T],
                                                           image.to_broadcast([128 - r0, 4, NIP]),
                                                           own.to_broadcast([128 - r0, 4, NIP]), ALU.mult)
                            last.then_inc(S["kbd_done"], 1)
                        elif kind == "vip":
                            v.tensor_copy(vip_sb[:, :], take(name)[0:GB * NIP, 0:C]).then_inc(S["vip_done"], 1)
                        elif kind == "ctx1":
                            ps = take(name)
                            dve.wait_ge(S["gram_done"], i + 1)
                            if i >= 2:
                                dve.wait_ge(S["pv_done"], NL0 + W1 * (i - 1))
                            for h in range(2):
                                v.tensor_copy(gv[:, i % 2, :, (D1 + GS) * h:(D1 + GS) * h + D1],
                                              ps[0:TT, TS:TS + C].rearrange("p (q h d) -> p q h d", h=2, d=D1)[:, :, h, :])
                            v.tensor_tensor(vbd_sb[:, i, :, :],
                                            ps[0:H * NIP, TS + C:TS + 2 * C].rearrange("p (h d) -> p h d", d=D1),
                                            own_head[:, :, :], ALU.mult).then_inc(S["gv_done"], 1)
                        elif kind == "ip":
                            v.tensor_tensor(o1b, take(name)[:, 0:C], o1[:, i % 2, :, :].rearrange("p h d -> p (h d)"),
                                            ALU.add).then_inc(S["o1_done"], 1)
                        elif kind == "y":
                            ps = take(name)
                            dve.wait_ge(S["bias_added"], NORMS.index((3, i // HB)) + 1)
                            v.tensor_tensor(xres[:, i, :], ps[:, 0:C], xres[:, i, :], ALU.add).then_inc(S["y_done"], 1)

                    def softmax_in(n):
                        dve.wait_ge(S["s_done"], n + 1)
                        if n < NL0:
                            J = step = K0[n // U0]
                            e = SE[:, n % 3, 0:4 * J]
                        else:
                            J, step = TT, T
                            e = SE1[:, n % 5, :]
                        sc = PS[n % 2][:, 0:4 * step].rearrange("p (i j) -> p i j", j=step)
                        v.tensor_reduce(mx[:, n % 2, :], sc[:, :, 0:J], AX, ALU.max).then_inc(S["mx_done"], 1)
                        dve.wait_ge(S["mx_done"], n + 1)
                        if n < NL0:
                            if n >= 3:
                                dve.wait_ge(S["pt_done"], n - 2)
                        else:
                            dve.wait_ge(S["pt_done"], max(NL0, n - 4))
                            if n - NL0 >= 5:
                                dve.wait_ge(S["gp_done"], n - NL0 - 4)
                        last = v.tensor_tensor(e.rearrange("p (i j) -> p i j", j=J), sc[:, :, 0:J],
                                               mx[:, n % 2, :].unsqueeze(2).to_broadcast([128, 4, J]), ALU.subtract)
                        if n >= NL0:
                            b, w = (n - NL0) // W1, (n - NL0) % W1
                            last = v.tensor_copy(sip[:, b % 3, 4 * w:4 * w + 4, :], sc[:, :, TT:T])
                        last.then_inc(S["sub_done"], 1)

                    def unit_out(n):
                        dve.wait_ge(S["pv_done"], n + 1)
                        PV = pv_bank(n)
                        if n < NL0:
                            o = PV[:, 0:4 * (DH + 1)].rearrange("p (i d) -> p i d", d=DH + 1)
                            v.reciprocal(rs[:, n % 2, :].unsqueeze(2), o[:, :, DH:DH + 1]).then_inc(S["rs_done"], 1)
                            dve.wait_ge(S["rs_done"], n + 1)
                            if n >= 2:
                                dve.wait_ge(S["ot_done"], n - 1)
                            v.tensor_tensor(ON[:, n % 2, :].rearrange("p (i d) -> p i d", d=DH), o[:, :, 0:DH],
                                            rs[:, n % 2, :].unsqueeze(2).to_broadcast([128, 4, DH]), ALU.mult)\
                                .then_inc(S["on_done"], 1)
                            return
                        b, w = (n - NL0) // W1, (n - NL0) % W1
                        o = PV[:, 0:4 * GV].rearrange("p (i d) -> p i d", d=GV)
                        r = rr[:, b % 2, 4 * w:4 * w + 4]
                        v.reciprocal(r.unsqueeze(2), o[:, :, D1 + T:D1 + T + 1]).then_inc(S["rs_done"], 1)
                        dve.wait_ge(S["rs_done"], n + 1)
                        for h in range(2):
                            pv = PV[:, 0:4 * GV].rearrange("p (q d) -> p q d", d=2 * GV)\
                                [:, :, (2 * GV - D1) * h:(2 * GV - D1) * h + D1]
                            v.tensor_tensor(o1[:, b % 2, 4 * w + h:4 * w + 3 + h:2, :], pv,
                                            r[:, h:3 + h:2].unsqueeze(2).to_broadcast([128, 2, D1]), ALU.mult)
                        v.tensor_tensor(sem4[:, b % 2, 4 * w:4 * w + 4, :], o[:, :, D1 + TT:D1 + T],
                                        r.unsqueeze(2).to_broadcast([128, 4, NIP]), ALU.mult).then_inc(S["on_done"], 1)

                    def gram_sum(n):
                        b, w = (n - NL0) // W1, (n - NL0) % W1
                        dve.wait_ge(S["gp_done"], n - NL0 + 1)
                        v.tensor_reduce(qq[:, b % 2, 4 * w:4 * w + 4], gs[n % 2], AX, ALU.add).then_inc(S["qq_done"], 1)

                    def image_scores(b):
                        k, e = b % 2, sip[:, b % 3, :, :]
                        dve.wait_ge(S["n20_done"], b + 1)
                        then(v.tensor_tensor(r20[:, 1, :], r20[:, 0, :], rr[:, k, :], ALU.mult))
                        then(v.tensor_scalar(r20[:, 2, :], r20[:, 1, :], EPS_L2, None, ALU.max))
                        then(v.reciprocal(r20[:, 3, :], r20[:, 2, :]))
                        then(v.scalar_tensor_tensor(sem4[:, k, :, :], sem4[:, k, :, :], SEM_SCALE,
                                                    r20[:, 3, :].unsqueeze(2).to_broadcast([128, H, NIP]), ALU.mult, ALU.mult))
                        then(v.scalar_tensor_tensor(e, e, SCALE1, sem4[:, k, :, :], ALU.mult, ALU.add))
                        then(v.tensor_reduce(r20[:, 1, :], e, AX, ALU.max))
                        v.tensor_tensor(e, e, r20[:, 1, :].unsqueeze(2).to_broadcast([128, H, NIP]), ALU.subtract)\
                            .then_inc(S["sip_done"], 1)

                    def image_probs(b):
                        e = sip[:, b % 3, :, :]
                        dve.wait_ge(S["sipe_done"], b + 1)
                        then(v.tensor_reduce(r20[:, 2, :], e, AX, ALU.add))
                        then(v.reciprocal(r20[:, 3, :], r20[:, 2, :]))
                        then(v.tensor_scalar(r20[:, 2, :], r20[:, 3, :], fside[:, 0:1], None, ALU.mult))
                        v.tensor_tensor(e, e, r20[:, 2, :].unsqueeze(2).to_broadcast([128, H, NIP]), ALU.mult)\
                            .then_inc(S["mask_done"], 1)

                    for s in range(FIRST, LAST):
                        for name in early_jobs(s):
                            job(name)
                        for k, h in norms_at(s):
                            if k < 3:
                                norm_stats(k, h)
                        if unit_at(s - 3) is not None:
                            unit_out(unit_at(s - 3))
                        if unit_at(s) is not None:
                            softmax_in(unit_at(s))
                        for k, h in norms_at(s):
                            if k < 3:
                                norm_out(k, h)
                        if l1_unit(s - 4) is not None:
                            gram_sum(l1_unit(s - 4))
                        for b in range(GB):
                            if s == TAIL_SLOT[b]:
                                image_scores(b)
                            if s == TAIL_SLOT[b] + 1:
                                image_probs(b)
                        for name in mid_jobs(s):
                            job(name)
                        if s == FIRST:
                            context_scale()
                        for name in late_jobs(s):
                            job(name)
                        for k, h in norms_at(s):
                            if k == 3:
                                l1_input(h)

                @block.gpsimd
                def _(pool):
                    g = nc.gpsimd
                    own = [0]

                    def then(ins):
                        own[0] += 1
                        ins.then_inc(S["pool_own"], 1)
                        pool.wait_ge(S["pool_own"], own[0])

                    def rstd_of(k, h):
                        pool.wait_ge(S["ln_stats"], REAL_NORMS.index((k, h)) + 1)
                        then(g.tensor_scalar(vp[:, :].unsqueeze(2), mv[:, :, 1:2], EPS_LN, None, ALU.add))
                        g.tensor_tensor(rstd[:, :], vp[:, :], p_mhalf[:, 0:HB], ALU.pow).then_inc(S["rstd_done"], 1)

                    def add_bias(k, h):
                        x = xres[:, HB * h:HB * h + HB, :]
                        if k == 0:
                            pool.wait_ge(S["x_in"], 16)
                        elif k < 3:
                            pool.wait_ge(S["ln_t"], REAL_NORMS.index((k, h)) + 1)
                        else:
                            pool.wait_ge(S["nx_done"], NORMS.index((k, h)) + 1)
                        g.tensor_tensor(x, xin[:, HB * h:HB * h + HB, :] if k == 0 else x,
                                        bias[:, k, :].unsqueeze(1).to_broadcast([128, HB, C]), ALU.add)\
                            .then_inc(S["bias_added"], 1)

                    def add_out(n):
                        a, h = n // U0, n // NP % 2
                        pool.wait_ge(S["wos_done"], n + 1)
                        if n % NP == 0:
                            pool.wait_ge(S["bias_added"], NORMS.index((a, h)) + 1)
                        if n >= 1:
                            pool.wait_ge(S["x_done"], n)
                        x = xres[:, HB * h:HB * h + HB, :]
                        g.tensor_tensor(x, x, WOs[:, n % 2, :, :], ALU.add).then_inc(S["x_done"], 1)

                    def gram_times_probs(n):
                        pool.wait_ge(S["gs_done"], n - NL0 + 1)
                        g.tensor_tensor(gs[n % 2], gs[n % 2], SE1[:, n % 5, :].rearrange("p (i j) -> p i j", j=TT),
                                        ALU.mult).then_inc(S["gp_done"], 1)

                    for s in range(FIRST, LAST):
                        for k, h in norms_at(s):
                            if k < 3:
                                rstd_of(k, h)
                            add_bias(k, h)
                        if s == FIRST:
                            pool.wait_ge(S["c_sq"], GB)
                            g.tensor_tensor(cst[:, 1, :], cst[:, 0, :], p_half[0:TS, 0:GB], ALU.pow).then_inc(S["c_pow"], 1)
                            pool.wait_ge(S["c_pow"], 1)
                            for i in range(2):
                                g.memset(qk[DH:128, i, 1, :], 0.0).then_inc(S["k_zero"], 1)
                                pool.wait_ge(S["k_zero"], 2 * i + 1)
                                g.memset(qk[0:DH, i, 2, :], 0.0).then_inc(S["k_zero"], 1)
                                pool.wait_ge(S["k_zero"], 2 * i + 2)
                        if l0_unit(s - 6) is not None:
                            add_out(l0_unit(s - 6))
                        if l1_unit(s - 3) is not None:
                            gram_times_probs(l1_unit(s - 3))
                        for b in range(GB):
                            if s == TAIL_SLOT[b] - 2:
                                pool.wait_ge(S["qq_done"], W1 * (b + 1))
                                g.tensor_tensor(r20[:, 0, :], qq[:, b % 2, :], p_half[:, :], ALU.pow).then_inc(S["n20_done"], 1)

            nc.sync.sem_clear(range(nums[0], nums[-1] + 1))
            nc.all_engine_barrier()


_INS = ['x', 'ctx_2048', 'fside_S_0',
        'L0_xattn_a1_wq', 'L0_xattn_a1_wk', 'L0_xattn_a1_wv', 'L0_xattn_a1_wo', 'L0_xattn_a1_bo',
        'L0_xattn_a2_wq', 'L0_xattn_a2_wk', 'L0_xattn_a2_wv', 'L0_xattn_a2_wo', 'L0_xattn_a2_bo',
        'L0_xattn_ff_w1', 'L0_xattn_ff_b1', 'L0_xattn_ff_w2', 'L0_xattn_ff_b2',
        'L0_xattn_ln1_g', 'L0_xattn_ln1_b', 'L0_xattn_ln2_g', 'L0_xattn_ln2_b', 'L0_xattn_ln3_g', 'L0_xattn_ln3_b',
        'L1_xattn_W_q', 'L1_xattn_W_k', 'L1_xattn_W_v', 'L1_xattn_W_k_ip', 'L1_xattn_W_v_ip', 'L1_xattn_W_out',
        'L1_xattn_b_out']


def kernel(**inputs):
    import numpy as _np
    import concourse.bacc as _bacc
    from concourse import mybir as _mybir
    from concourse.bass_utils import run_bass_kernel_spmd as _run

    nc = _bacc.Bacc("TRN2", target_bir_lowering=False, num_devices=1, dynamic_dma_scratch_size=1024)
    arrays, aps = {}, {}
    for name in _INS:
        a = _np.ascontiguousarray(inputs[name])
        arrays[f"in_{name}_dram"] = a
        aps[name] = nc.dram_tensor(f"in_{name}_dram", a.shape, _mybir.dt.from_np(a.dtype), kind="ExternalInput").ap()
    out = nc.dram_tensor("out_dram", inputs["x"].shape, _mybir.dt.float32, kind="ExternalOutput").ap()
    xattn_program(nc, aps, out)
    r = _run(nc, [arrays], core_ids=[0])
    return r.results[0]["out_dram"]
```

```python
import concourse.bass as bass
from concourse import mybir
from contextlib import ExitStack



def xattn_program(nc: bass.Bass, D, out: bass.AP):
    fp32 = mybir.dt.float32
    f32r = mybir.dt.float32r
    ALU = mybir.AluOpType
    ACT = mybir.ActivationFunctionType
    AX = mybir.AxisListType.X

    x_dram, ctx_dram = D["x"], D["ctx_2048"]
    B, N, C = x_dram.shape
    T, E = ctx_dram.shape[1:]
    H, DH = 20, 64
    INNER = H * DH
    FF = 4 * C
    GB = 4
    GROUPS = B // GB
    NP = H // 2
    HB = GB // 2
    HT = HB * 128
    U0 = NP * 2
    M = C - 128
    NIP = 4
    TT = T - NIP
    TS = T + NIP + 1
    D1 = C // H
    GS = TT + NIP + 1
    GV = GS + 2 * D1
    W1 = 5
    SCALE0, SCALE1 = DH ** -0.5, D1 ** -0.5
    SEM_SCALE, EPS_LN, EPS_L2 = 0.5, 1e-5, 1e-12
    K0 = [N, T]
    NL0 = 2 * U0
    F = FF // 128

    L1_SLOT = [0, 2, 3, 5, 6, 8, 9, 11, 12, 14, 18, 21, 24, 27, 30, 33, 38, 41, 44, 47]
    FIRST, LAST = -1, 65
    UNIT = {}
    for s in range(60):
        UNIT[s] = NL0 + L1_SLOT.index(s) if s in L1_SLOT else s - sum(x < s for x in L1_SLOT)
    SLOT = {n: s for s, n in UNIT.items()}

    NORM_SLOT = {(2, 1): 0, (3, 1): 8, (0, 1): 12, (1, 0): SLOT[9] + 8, (1, 1): SLOT[19] + 6,
                 (2, 0): SLOT[29] + 5, (3, 0): 60, (0, 0): 61}
    FF_SLOT = [57, 57, 58, 58, 59] + [3, 3, 5, 5, 7]
    Q1_SLOT = [62, 10]
    PREP_SLOT = [26, 31]
    VIP_SLOT = 53
    K1_SLOT = {0: (50, 52), 1: (15, 16)}
    CTX1_SLOT = {0: 54, 1: 61, 2: 17, 3: 26}
    LONE_L1_SLOT = list(range(0, 10)) + list(range(16, 26))
    LONE_K1_SLOT = {1: (10, 11)}
    LONE_CTX1_SLOT = {2: 15, 3: 20}


    ctx = ExitStack()
    with ctx:
        def sb(name, shape, dt=fp32):
            return ctx.enter_context(nc.sbuf_tensor(name, shape, dt))

        def split_weights(name, n):
            return (sb(name + "_hi", [128, n], f32r), sb(name + "_lo", [128, n], f32r),
                    sb(name + "_rem", [128, n], f32r))

        w_q = [split_weights("w_q0", INNER), split_weights("w_q1", INNER)]
        w_k0 = split_weights("w_k0", INNER)
        w_v0 = split_weights("w_v0", INNER)
        w_kc = sb("w_kc", [128, 2, 2, INNER], f32r)
        w_vc = sb("w_vc", [128, 2, 2, INNER], f32r)
        w_o = [sb("w_o0", [128, NP, C]), sb("w_o1", [128, NP, C])]
        w_1 = split_weights("w_1", 2 * FF)
        w_2 = sb("w_2", [128, FF // 128, C])
        w_q1 = split_weights("w_q1h", C)
        w_k1 = sb("w_k1h", [128, 2, 2, C], f32r)
        w_v1 = sb("w_v1h", [128, 2, 2, C], f32r)
        w_kip = sb("w_kip", [128, 2, C])
        w_vip = sb("w_vip", [128, 2, C])
        w_out = sb("w_out", [128, C])
        small = sb("small", [128, C])
        ln_g = sb("ln_g", [128, 3, C])
        ln_b = sb("ln_b", [128, 3, C])
        bias = sb("bias", [128, 4, C])
        b_1 = sb("b_1", [128, 2 * FF // 128])
        fside = sb("fside", [128, 1])
        ident = sb("ident", [128, 128])
        is_ip = sb("is_ip", [TS, 1])
        not_ip = sb("not_ip", [TS, 1])
        head_of_row = sb("head_of_row", [128, 4])
        own_head = small[0:H * NIP, :].rearrange("p (h d) -> p h d", d=D1)
        pick = sb("pick", [GB * NIP, GB, H * NIP])
        p_half = sb("p_half", [128, H])
        p_mhalf = sb("p_mhalf", [128, GB])
        xres = sb("xres", [128, GB, C])
        x1 = sb("x1", [128, GB, C])
        shared = sb("shared", [128, HB, E])
        cin, gl = shared[0:TS, :, :], shared[:, :, :]
        cT = sb("cT", [128, 2, 2, GB * TS], f32r)
        cipT = sb("cipT", [128, 2, GB * NIP])
        cst = sb("cst", [TS, 4, HB])
        lt = sb("lt", [128, HB, C])
        nx = sb("nx", [128, HB, 256])
        nT = sb("nT", [128, 2, 3, HT], f32r)
        st6 = sb("st6", [128, HB, 6])
        mv = sb("mv", [128, HB, 2])
        rstd = sb("rstd", [128, HB])
        vp = sb("vp", [128, HB])
        qk = sb("qk", [128, 2, 3, HT])
        v_sb = sb("v_sb", [128, 2, HB, 4, DH + 1])
        SE = sb("SE", [128, 3, 512])
        PTs = sb("PTs", [128, 2, 512])
        work = sb("work", [128, 1024])
        ON = work[:, 0:512].rearrange("p (i n) -> p i n", i=2)
        OTs = work[:, 512:1024].rearrange("p (i n) -> p i n", i=2)
        WOs = sb("WOs", [128, 2, HB, C])
        mx = sb("mx", [128, 2, 4])
        rs = sb("rs", [128, 2, 4])
        hT = sb("hT", [128, 2, HT])
        kbd = sb("kbd", [128, 2, HB, 4, T])
        q1T = sb("q1T", [128, 2, 2, HT])
        vip_sb = sb("vip_sb", [GB * NIP, C])
        vbd_sb = sb("vbd_sb", [H * NIP, 2, H, D1])
        gv = sb("gv", [TT, 2, NP, GV])
        sip = sb("sip", [128, 2, H, NIP])
        qq = sb("qq", [128, 2, H])
        rr = sb("rr", [128, 2, H])
        r20 = sb("r20", [128, 4, H])
        o1 = sb("o1", [128, 2, H, D1])
        sem4 = sb("sem4", [128, 2, H, NIP])
        ipTs = sb("ipTs", [H * NIP, 128])
        o1T = sb("o1T", [128, 256])
        own16 = r20[:, 0, 0:16]
        csq = nx[0:TS, 0, :]

        PG = [ctx.enter_context(nc.psum_tensor(f"PG{i}", [128, 512], fp32)) for i in range(3)]
        PS = [ctx.enter_context(nc.psum_tensor(f"PS{i}", [128, 512], fp32)) for i in range(2)]
        PT = ctx.enter_context(nc.psum_tensor("PT", [128, 512], fp32))
        PVS = [ctx.enter_context(nc.psum_tensor(f"PV{i}", [128, 512], fp32)) for i in range(2)]

        def sem(name):
            return ctx.enter_context(nc.semaphore(name))

        stage_in = [sem("stage_in0"), sem("stage_in1")]
        stage_used = sem("stage_used")
        plain_in = sem("plain_in")
        hi_done = sem("hi_done")
        setup_pool = sem("setup_pool")

        SPLITS = []
        for name, tiles in (("L0_xattn_a1_wq", w_q[0]), ("L0_xattn_a1_wk", w_k0), ("L0_xattn_a1_wv", w_v0),
                            ("L0_xattn_a2_wq", w_q[1]), ("L0_xattn_ff_w1", w_1), ("L1_xattn_W_q", w_q1)):
            n = D[name].shape[1]
            SPLITS.append(([(D[name][0:128, :], 0, 128)], tiles[0][:, :], tiles[1][:, :], n))
            SPLITS.append(([(D[name][128:C, :], M * r, M * r + M) for r in range(4)], tiles[2][:, :], None, n))
        for name, tile in (("L0_xattn_a2_wk", w_kc), ("L0_xattn_a2_wv", w_vc),
                           ("L1_xattn_W_k", w_k1), ("L1_xattn_W_v", w_v1)):
            n = D[name].shape[1]
            for c in range(2):
                SPLITS.append(([(D[name][128 * c:128 * c + 128, :], 0, 128)], tile[:, c, 0, :], tile[:, c, 1, :], n))
        stage = [SE[:, :, :].rearrange("p a b -> p (a b)"), qk[:, :, :, :].rearrange("p a i b -> p (a i b)")]

        PLAIN = []
        for a, w in enumerate(("L0_xattn_a1_wo", "L0_xattn_a2_wo")):
            PLAIN.append((w_o[a][:, :, :], D[w].rearrange("(p k) n -> k p n", k=128)))
        PLAIN.append((w_2[:, :, :], D["L0_xattn_ff_w2"].rearrange("(p k) n -> k p n", k=128)))
        for w, t in (("L1_xattn_W_k_ip", w_kip), ("L1_xattn_W_v_ip", w_vip)):
            PLAIN.append((t[:, :, :], D[w].rearrange("(c k) n -> k c n", k=128)))
        PLAIN.append((w_out[:, :], D["L1_xattn_W_out"][0:128, :]))
        PLAIN.append((small[96:128, :], D["L1_xattn_W_out"][128:C, :]))
        for k in range(3):
            PLAIN.append((ln_g[:, k, :], D[f"L0_xattn_ln{k + 1}_g"].partition_broadcast(128)))
            PLAIN.append((ln_b[:, k, :], D[f"L0_xattn_ln{k + 1}_b"].partition_broadcast(128)))
        for k, w in enumerate(("L0_xattn_a1_bo", "L0_xattn_a2_bo", "L0_xattn_ff_b2", "L1_xattn_b_out")):
            PLAIN.append((bias[:, k, :], D[w].partition_broadcast(128)))
        PLAIN.append((b_1[:, :], D["L0_xattn_ff_b1"].rearrange("(t p) -> p t", p=128)))
        PLAIN.append((fside[:, :], D["fside_S_0"].rearrange("(p a) -> p a", a=1)))

        with nc.Block() as block:
            @block.sync
            def _(sp):
                count = [0, 0]
                for i, (parts, _, _, n) in enumerate(SPLITS):
                    if i >= 2:
                        sp.wait_ge(stage_used, i - 1)
                    for src, p0, p1 in parts:
                        sp.dma_start(stage[i % 2][p0:p1, 0:n], src).then_inc(stage_in[i % 2], 16)

            @block.scalar
            def _(act):
                for dst, src in PLAIN:
                    act.dma_start(dst, src, allow_slow_non_contiguous=True).then_inc(plain_in, 16)
                count = [0, 0]
                for i, (parts, hi, lo, n) in enumerate(SPLITS):
                    count[i % 2] += 16 * len(parts)
                    act.wait_ge(stage_in[i % 2], count[i % 2])
                    nc.scalar.activation(hi, stage[i % 2][:, 0:n], mybir.ActivationFunctionType.Copy)\
                        .then_inc(hi_done, 1)
                act.wait_ge(plain_in, 16 * len(PLAIN))

            @block.vector
            def _(dve):
                for i, (parts, hi, lo, n) in enumerate(SPLITS):
                    s = stage[i % 2]
                    dve.wait_ge(hi_done, i + 1)
                    if lo is not None:
                        nc.vector.tensor_tensor(lo, s[:, 0:n], hi.bitcast(fp32), ALU.subtract).then_inc(stage_used, 1)
                    else:
                        nc.vector.tensor_tensor(hi[M:2 * M], s[M:2 * M, 0:n], hi[M:2 * M].bitcast(fp32), ALU.subtract)
                        nc.vector.tensor_tensor(hi[3 * M:4 * M], s[3 * M:4 * M, 0:n], hi[3 * M:4 * M].bitcast(fp32),
                                                ALU.subtract).then_inc(stage_used, 1)
                dve.wait_ge(stage_used, len(SPLITS))
                nc.vector.memset(v_sb[:, :, :, :, :], 1.0)
                nc.vector.memset(gv[:, :, :, :], 1.0)
                nc.vector.memset(qk[:, :, :, :], 0.0)

            @block.gpsimd
            def _(pool):
                g = nc.gpsimd
                steps = [0]

                def done(ins):
                    steps[0] += 1
                    ins.then_inc(setup_pool, 1)
                    pool.wait_ge(setup_pool, steps[0])

                g.memset(p_half[:, :], 0.5)
                g.memset(p_mhalf[:, :], -0.5)
                done(g.memset(cin[:, :, :], 0.0))
                done(g.memset(ident[:, :], 0.0))
                done(g.affine_select(out=ident[:, :], in_=ident[:, :], compare_op=ALU.not_equal, fill=1.0,
                                     base=0, pattern=[[-1, 128]], channel_multiplier=1))
                done(g.memset(is_ip[:, :], 1.0))
                done(g.affine_select(out=is_ip[:, :], in_=is_ip[:, :], compare_op=ALU.is_ge, fill=0.0,
                                     base=-T, pattern=[[0, 1]], channel_multiplier=1))
                done(g.tensor_scalar(not_ip[:, :], is_ip[:, :], -1.0, 1.0, ALU.mult, ALU.add))
                done(g.memset(own16, 1.0))
                done(g.affine_select(out=own16, in_=own16, compare_op=ALU.is_ge, fill=0.0,
                                     base=0, pattern=[[-D1, 16]], channel_multiplier=1))
                done(g.affine_select(out=own16, in_=own16, compare_op=ALU.is_ge, fill=0.0,
                                     base=D1 - 1, pattern=[[D1, 16]], channel_multiplier=-1))
                done(g.tensor_tensor(head_of_row[:, :], own16[:, 0:4], own16[:, 4:8], ALU.add))
                done(g.tensor_tensor(head_of_row[:, :], head_of_row[:, :], own16[:, 8:12], ALU.add))
                done(g.tensor_tensor(head_of_row[:, :], head_of_row[:, :], own16[:, 12:16], ALU.add))
                done(g.memset(own_head, 1.0))
                done(g.affine_select(out=own_head, in_=own_head, compare_op=ALU.is_ge, fill=0.0,
                                     base=0, pattern=[[-NIP, H], [0, D1]], channel_multiplier=1))
                done(g.affine_select(out=own_head, in_=own_head, compare_op=ALU.is_ge, fill=0.0,
                                     base=NIP - 1, pattern=[[NIP, H], [0, D1]], channel_multiplier=-1))
                pk = pick[:, :, :].rearrange("p b (h n) -> p b h n", n=NIP)
                done(g.memset(pick[:, :, :], 0.0))
                done(g.affine_select(out=pk, in_=pk, compare_op=ALU.not_equal, fill=1.0, base=0,
                                     pattern=[[-NIP, GB], [0, H], [-1, NIP]], channel_multiplier=1))

        names = ["x_in0", "x_in1", "c_in", "out_done0", "out_done1", "job_full",
                 "ln_stats", "ln_t", "rstd_done", "nx_done", "nT_act", "nT_dve", "bias_added",
                 "c_sq", "c_pow", "c_dve", "cT_act", "cT_dve",
                 "qk_done", "v_done",
                 "s_done", "mx_done", "sub_done", "exp_done", "pt_done", "pts_done", "pv_done", "rs_done",
                 "on_done", "ots_done", "wos_done", "x_done",
                 "gelu_done", "h_done", "down_added",
                 "q1_done", "kbd_done", "vip_done", "gram_done", "gv_done",
                 "qq_done", "n20_done", "d_chain", "tail_part", "sip_done", "sipe_done", "mask_done",
                 "ipT_done", "o1_done", "o1T_done", "y_done", "pool_own"]
        S = {n: sem(n) for n in names}
        nums = sorted(x.num for x in S.values())
        assert nums == list(range(nums[0], nums[0] + len(nums)))

        def group_step(has_l0, has_l1, has_next, x_in, c_in, x_next, y_out):
            l1_slot = L1_SLOT if has_l0 else LONE_L1_SLOT
            units = UNIT if has_l0 else {s: NL0 + i for i, s in enumerate(LONE_L1_SLOT)}
            k1_slot = K1_SLOT if has_l0 else LONE_K1_SLOT
            ctx1_slot = CTX1_SLOT if has_l0 else LONE_CTX1_SLOT
            tail_slot = [l1_slot[W1 * b + W1 - 1] + 5 for b in range(GB)]

            def unit_at(s):
                n = units.get(s)
                return n if n is not None and (has_l0 if n < NL0 else has_l1) else None

            def l0_unit(s):
                n = unit_at(s)
                return n if n is not None and n < NL0 else None

            def owner(k, h):
                return has_l1 if k >= 2 and h == 1 else has_next if (k, h) == (0, 0) else has_l0

            NORMS = [kh for kh in NORM_SLOT if owner(*kh)]
            REAL_NORMS = [kh for kh in NORMS if kh[0] < 3]

            def norms_at(s):
                return [kh for kh in NORMS if NORM_SLOT[kh] == s]

            def preps_at(s):
                return [h for h in range(2) if has_l0 and PREP_SLOT[h] == s]

            PLACE = {n: i for i, n in enumerate(unit_at(s) for s in sorted(units) if unit_at(s) is not None)}

            def mid_jobs(s):
                return [(kind, l0_unit(s + d)) for kind, d in (("qk", 2), ("wo", -5), ("ot", -4)) if l0_unit(s + d) is not None]

            def late_jobs(s):
                n = l0_unit(s - 1)
                jobs = [("v", n // 2)] if n is not None and n % 2 == 0 else []
                jobs += [("q1", h) for h in range(2) if s == Q1_SLOT[h] and owner(3, h)]
                jobs += [("xT",) + kh for kh in NORMS if s == NORM_SLOT[kh] + (1 if kh[0] == 3 else 2)]
                jobs += [("cT", h) for h in preps_at(s - 1)]
                jobs += [(kind, b) for b in range(GB) for d, kind in ((5, "ipT"), (6, "ip"), (7, "oT1"), (8, "y"))
                         if has_l1 and s == tail_slot[b] + d]
                for h in range(2):
                    if has_l1 if h else has_l0:
                        tiles = range(F * h, F * h + F)
                        jobs += [("down", i) for i in tiles if FF_SLOT[i] + 1 == s]
                        jobs += [("ff", i) for i in tiles if FF_SLOT[i] == s]
                    if has_l1 if h else has_l0:
                        jobs += [("k1", r, h) for r in range(2) if s == k1_slot[h][r]]
                if has_l0 and s == VIP_SLOT:
                    jobs.append(("vip", 0))
                jobs += [("ctx1", b) for b in range(GB) if (has_l1 if b >= HB else has_l0) and ctx1_slot[b] == s]
                return jobs

            JOBS = [j for s in range(FIRST, LAST) for j in mid_jobs(s) + late_jobs(s)]
            JOB = {name: n for n, name in enumerate(JOBS)}

            def nth(name):
                return sum(j[0] == name[0] for j in JOBS[:JOB[name] + 1])

            def read_out(name):
                last_read = {"xT": "nT_dve", "qk": "qk_done", "ot": "ots_done", "wo": "wos_done", "v": "v_done", "cT": "cT_dve", "ff": "h_done",
                             "down": "down_added", "q1": "q1_done", "k1": "kbd_done", "vip": "vip_done",
                             "ctx1": "gv_done", "ipT": "ipT_done", "ip": "o1_done", "oT1": "o1T_done", "y": "y_done"}
                return S[last_read[name[0]]], nth(name)

            def bank(name):
                return PG[JOB[name] % len(PG)]

            with nc.Block() as block:

                def wait_gv_used(engine, b):
                    if has_l1:
                        engine.wait_ge(S["pv_done"], PLACE[NL0 + W1 * ((b + 2) % GB) + W1 - 1] + 1)

                @block.sync
                def _(sp):
                    def load_context(h):
                        for rows, t0, t1 in ((slice(0, T), 0, T), (slice(T, T + NIP), TT, T)):
                            sp.dma_start(cin[rows, :, :], c_in[HB * h:HB * h + HB, t0:t1, :].rearrange("b t e -> t b e"))\
                                .then_inc(S["c_in"], 16)

                    def store(b):
                        sp.wait_ge(S["y_done"], b + 1)
                        sp.dma_start(y_out[b], x1[:, b, :]).then_inc(S[f"out_done{b // HB}"], 16)

                    def load_x(x, h):
                        sp.dma_start(xres[:, HB * h:HB * h + HB, :], x[HB * h:HB * h + HB].rearrange("b n c -> n b c"))\
                            .then_inc(S[f"x_in{h}"], 16)

                    if has_l0:
                        if has_l1:
                            sp.wait_ge(S["down_added"], nth(("down", F)))
                        load_x(x_in, 1)
                        if has_l1:
                            sp.wait_ge(S["h_done"], nth(("ff", 2 * F - 1)))
                        load_context(0)
                    if has_l1:
                        store(0)
                    if has_l0:
                        sp.wait_ge(S["job_full"], JOB[("cT", 0)] + 1)
                        load_context(1)
                    if has_l1:
                        store(1)
                        store(2)
                    if has_next:
                        if has_l0:
                            sp.wait_ge(S["down_added"], nth(("down", 0)))
                        load_x(x_next, 0)
                    if has_l1:
                        store(3)
                        for h in range(2):
                            sp.wait_ge(S[f"out_done{h}"], 16 * HB)

                @block.tensor
                def _(pe):
                    mm = nc.tensor.matmul
                    tr = nc.tensor.transpose
                    SPLIT3 = [(0, 0), (0, 1), (1, 0)]

                    def rows160(ps, w, c0, h):
                        mm(ps, w[0][:, c0:c0 + 128], nT[:, h, 0, :], start=True, stop=False)
                        mm(ps, w[1][:, c0:c0 + 128], nT[:, h, 0, :], start=False, stop=False)
                        mm(ps, w[0][:, c0:c0 + 128], nT[:, h, 2, :], start=False, stop=False)
                        return mm(ps, w[2][:, c0:c0 + 128], nT[:, h, 1, :], start=False, stop=True)

                    def rows160_out(ps, w, c0, n, h, b):
                        t = slice(128 * b, 128 * b + 128)
                        mm(ps, nT[:, h, 0, t], w[0][:, c0:c0 + n], start=True, stop=False)
                        mm(ps, nT[:, h, 0, t], w[1][:, c0:c0 + n], start=False, stop=False)
                        mm(ps, nT[:, h, 2, t], w[0][:, c0:c0 + n], start=False, stop=False)
                        return mm(ps, nT[:, h, 1, t], w[2][:, c0:c0 + n], start=False, stop=True)

                    def ctx_cols(ps, w, c0, h):
                        for c in range(2):
                            for i, (hw, hc) in enumerate(SPLIT3):
                                last = mm(ps, w[:, c, hw, c0:c0 + 128], cT[:, c, hc, HB * TS * h:HB * TS * (h + 1)],
                                          start=(c == 0 and i == 0), stop=(c == 1 and i == 2))
                        return last

                    def ctx_rows(ps, w, c0, n, b, rows):
                        for c in range(2):
                            for i, (hw, hc) in enumerate(SPLIT3):
                                last = mm(ps, cT[:, c, hc, TS * b:TS * b + rows], w[:, c, hw, c0:c0 + n],
                                          start=(c == 0 and i == 0), stop=(c == 1 and i == 2))
                        return last

                    def job(name):
                        kind, i = name[0], name[-1]
                        if JOB[name] >= len(PG):
                            pe.wait_ge(*read_out(JOBS[JOB[name] - len(PG)]))
                        ps = bank(name)
                        if kind == "cT":
                            pe.wait_ge(S["c_dve"], HB * (i + 1))
                            for c in range(2):
                                for b in range(HB):
                                    last = tr(ps[:, TS * (HB * c + b):TS * (HB * c + b + 1)],
                                              cin[:, b, 128 * c:128 * c + 128], ident[0:TS, 0:TS])
                        elif kind == "xT":
                            pe.wait_ge(S["nx_done"], NORMS.index(name[1:]) + 1)
                            for part in range(2):
                                for b in range(HB):
                                    last = tr(ps[:, HT * part + 128 * b:HT * part + 128 * b + 128],
                                              nx[:, b, 128 * part:128 * part + 128], ident[:, :])
                        elif kind == "qk":
                            a, h, p = i // U0, i // NP % 2, i % NP
                            if p == 0:
                                if i > 0:
                                    wait_nT(a, h)
                                if a == 1:
                                    pe.wait_ge(S["cT_act"], h + 1)
                                    pe.wait_ge(S["cT_dve"], h + 1)
                            rows160(ps[:, 0:HT], w_q[a], 128 * p, h)
                            if a == 0:
                                last = rows160(ps[:, HT:2 * HT], w_k0, 128 * p, h)
                            else:
                                last = ctx_cols(ps[:, HT:HT + HB * TS], w_kc, 128 * p, h)
                        elif kind == "ot":
                            pe.wait_ge(S["on_done"], PLACE[i] + 1)
                            for b in range(HB):
                                last = tr(ps[:, 128 * b:128 * b + 128], ON[:, i % 2, 128 * b:128 * b + 128], ident[:, :])
                        elif kind == "wo":
                            pe.wait_ge(S["ots_done"], i + 1)
                            for b in range(HB):
                                last = mm(ps[:, C * b:C * b + C], OTs[:, i % 2, 128 * b:128 * b + 128],
                                          w_o[i // U0][:, i % NP, :], start=True, stop=True)
                        elif kind == "v":
                            a, h, p = 2 * i // U0, 2 * i // NP % 2, 2 * i % NP
                            for b in range(HB):
                                o = ps[0:K0[a], 256 * b:256 * b + 256]
                                if a == 0:
                                    last = rows160_out(o, w_v0, 128 * p, 256, h, b)
                                else:
                                    last = ctx_rows(o, w_vc, 128 * p, 256, HB * h + b, T)
                        elif kind == "ff":
                            h, t = i // F, i % F
                            if t == 0:
                                wait_nT(2, h)
                            rows160(ps[:, 0:HT], w_1, FF + 128 * t, h)
                            last = rows160(ps[:, HT:2 * HT], w_1, 128 * t, h)
                        elif kind == "down":
                            pe.wait_ge(S["h_done"], nth(("ff", i)))
                            for b in range(HB):
                                last = mm(ps[:, C * b:C * b + C], hT[:, nth(name) % 2, 128 * b:128 * b + 128], w_2[:, i % F, :],
                                          start=True, stop=True)
                        elif kind == "q1":
                            wait_nT(3, i)
                            for r in range(2):
                                last = rows160(ps[:, HT * r:HT * r + HT], w_q1, M * r, i)
                        elif kind == "k1":
                            r, kw, iw = name[1], HB * TS, HB * NIP
                            ctx_cols(ps[:, 0:kw], w_k1, M * r, i)
                            for c in range(2):
                                last = mm(ps[:, kw:kw + iw], w_kip[:, c, M * r:M * r + 128],
                                          cipT[:, c, iw * i:iw * i + iw], start=(c == 0), stop=(c == 1))
                        elif kind == "vip":
                            for c in range(2):
                                last = mm(ps[0:GB * NIP, 0:C], cipT[:, c, :], w_vip[:, c, :], start=(c == 0), stop=(c == 1))
                        elif kind == "ctx1":
                            for c in range(2):
                                for j, (h0, h1) in enumerate(SPLIT3):
                                    mm(ps[0:TT, 0:TS], cT[:, c, h0, TS * i:TS * i + TT], cT[:, c, h1, TS * i:TS * i + TS],
                                       start=(c == 0 and j == 0), stop=(c == 1 and j == 2))
                            ctx_rows(ps[0:TT, TS:TS + C], w_v1, 0, C, i, TT)
                            if i < HB:
                                pe.wait_ge(S["vip_done"], 1)
                            last = mm(ps[0:H * NIP, TS + C:TS + 2 * C], pick[:, i, :], vip_sb[:, :], start=True, stop=True)
                        elif kind == "ipT":
                            pe.wait_ge(S["mask_done"], i + 1)
                            last = tr(ps[0:H * NIP, 0:128], sip[:, i % 2, :, :].rearrange("p h n -> p (h n)"), ident[:, :])
                        elif kind == "ip":
                            pe.wait_ge(S["ipT_done"], i + 1)
                            last = mm(ps[:, 0:C], ipTs[:, :], vbd_sb[:, i % 2, :, :].rearrange("p h d -> p (h d)"),
                                      start=True, stop=True)
                        elif kind == "oT1":
                            pe.wait_ge(S["o1_done"], i + 1)
                            o = o1[:, i % 2, :, :].rearrange("p h d -> p (h d)")
                            tr(ps[:, 0:128], o[:, 0:128], ident[:, :])
                            last = tr(ps[:, 128:256], o[:, M:C], ident[:, :])
                        elif kind == "y":
                            pe.wait_ge(S["o1T_done"], i + 1)
                            mm(ps[:, 0:C], o1T[:, 0:128], w_out[:, :], start=True, stop=False)
                            last = mm(ps[:, 0:C], o1T[96:128, 128:256], small[96:128, :], start=False, stop=True)
                        last.then_inc(S["job_full"], 1)

                    def wait_nT(k, h):
                        pe.wait_ge(S["nT_act"], NORMS.index((k, h)) + 1)
                        pe.wait_ge(S["nT_dve"], NORMS.index((k, h)) + 1)

                    def scores(n):
                        place = PLACE[n]
                        if place >= 2:
                            pe.wait_ge(S["sub_done"], place - 1)
                        ps = PS[place % 2]
                        if n < NL0:
                            J, kstep = (N, 128) if n < U0 else (T, TS)
                            pe.wait_ge(S["qk_done"], n + 1)
                            for b in range(HB):
                                last = mm(ps[:, 2 * J * b:2 * J * b + 2 * J], qk[:, n % 2, 0, 128 * b:128 * b + 128],
                                          qk[:, n % 2, 1:3, kstep * b:kstep * b + J], start=True, stop=True)
                        else:
                            b, w = (n - NL0) // W1, (n - NL0) % W1
                            h = b // HB
                            if w == 0 and h == 1:
                                pe.wait_ge(S["kbd_done"], nth(("k1", 1, 1)))
                            r, row = (0, 32 * w) if w < 4 else (1, 96)
                            last = mm(ps[:, 0:4 * T], q1T[row:row + 32, h, r, 128 * (b % HB):128 * (b % HB) + 128],
                                      kbd[row:row + 32, r, b % HB, :, :].rearrange("p h t -> p (h t)"),
                                      start=True, stop=True)
                        last.then_inc(S["s_done"], 1)

                    def probs_transposed(n):
                        place = PLACE[n]
                        pe.wait_ge(S["exp_done"], place + 1)
                        if place >= 1:
                            pe.wait_ge(S["pts_done"], place)
                        for i in range(4):
                            J = K0[n // U0] if n < NL0 else TT
                            last = tr(PT[0:J, 128 * i:128 * i + 128], SE[:, place % 3, J * i:J * i + J], ident[:, :])
                        last.then_inc(S["pt_done"], 1)

                    def probs_v(n):
                        place = PLACE[n]
                        pe.wait_ge(S["pts_done"], place + 1)
                        PV = PVS[place % 2]
                        if place >= 2:
                            pe.wait_ge(S["on_done"], place - 1)
                        if n < NL0:
                            pe.wait_ge(S["v_done"], n // 2 + 1)
                            J = K0[n // U0]
                            for i in range(4):
                                last = mm(PV[:, (DH + 1) * i:(DH + 1) * (i + 1)],
                                          PTs[0:J, place % 2, 128 * i:128 * i + 128],
                                          v_sb[0:J, n // 2 % 2, i // 2, 2 * (n % 2) + i % 2, :], start=True, stop=True)
                        else:
                            b, w = (n - NL0) // W1, (n - NL0) % W1
                            if w == 0 and b >= HB:
                                pe.wait_ge(S["gv_done"], nth(("ctx1", b)))
                                pe.wait_ge(S["gram_done"], nth(("ctx1", b)))
                            for i in range(4):
                                off = D1 * (i % 2)
                                last = mm(PV[:, GV * i + off:GV * i + off + GS + D1],
                                          PTs[0:TT, place % 2, 128 * i:128 * i + 128],
                                          gv[:, b % 2, 2 * w + i // 2, off:off + GS + D1], start=True, stop=True)
                        last.then_inc(S["pv_done"], 1)

                    for s in range(FIRST, LAST):
                        if unit_at(s + 1) is not None:
                            scores(unit_at(s + 1))
                        if unit_at(s - 1) is not None:
                            probs_transposed(unit_at(s - 1))
                        for name in mid_jobs(s):
                            job(name)
                        if unit_at(s - 2) is not None:
                            probs_v(unit_at(s - 2))
                        for name in late_jobs(s):
                            job(name)

                @block.scalar
                def _(act):
                    a_ = nc.scalar.activation

                    def take(name):
                        act.wait_ge(S["job_full"], JOB[name] + 1)
                        return bank(name)

                    def job(name):
                        kind, i = name[0], name[-1]
                        if kind == "cT":
                            w = HB * TS
                            a_(cT[:, :, 0, w * i:w * i + w], take(name)[:, 0:2 * w].rearrange("p (c n) -> p c n", c=2),
                               ACT.Copy).then_inc(S["cT_act"], 1)
                        elif kind == "xT":
                            a_(nT[:, i, 0:2, :].rearrange("p r n -> p (r n)"), take(name)[:, :], ACT.Copy)\
                                .then_inc(S["nT_act"], 1)
                        elif kind == "qk":
                            ps, kw = take(name), HT if i < U0 else HB * TS
                            a_(qk[:, i % 2, 0, :], ps[:, 0:HT], ACT.Copy)
                            for e in range(2):
                                last = a_(qk[DH * e:DH * e + DH, i % 2, 1 + e, 0:kw], ps[DH * e:DH * e + DH, HT:HT + kw],
                                          ACT.Copy)
                            last.then_inc(S["qk_done"], 1)
                        elif kind == "wo":
                            ps = take(name)
                            if i >= 2:
                                act.wait_ge(S["x_done"], i - 1)
                            a_(WOs[:, i % 2, :, :].rearrange("p b c -> p (b c)"), ps[:, 0:HB * C], ACT.Copy)\
                                .then_inc(S["wos_done"], 1)
                        elif kind == "ot":
                            ps = take(name)
                            if i >= 2:
                                act.wait_ge(S["job_full"], JOB[("wo", i - 2)] + 1)
                            a_(OTs[:, i % 2, :], ps[:, 0:HT], ACT.Copy).then_inc(S["ots_done"], 1)
                        elif kind == "ff":
                            h, t = i // F, i % F
                            ps = take(name)
                            if nth(name) > 2:
                                act.wait_ge(S["h_done"], nth(name) - 2)
                            a_(gl[:, nth(name) % 2, :], ps[:, 0:HT], ACT.Gelu, bias=b_1[:, F + t:F + t + 1])\
                                .then_inc(S["gelu_done"], 1)
                        elif kind == "q1":
                            a_(q1T[:, i, :, :].rearrange("p r n -> p (r n)"), take(name)[:, :], ACT.Copy)\
                                .then_inc(S["q1_done"], 1)
                        elif kind == "ctx1":
                            ps = take(name)
                            wait_gv_used(act, i)
                            a_(gv[:, i % 2, :, D1:D1 + TT], ps[0:TT, 0:TT].unsqueeze(1).to_broadcast([TT, NP, TT]), ACT.Copy)
                            a_(gv[:, i % 2, :, D1 + TT:D1 + T],
                               ps[0:TT, T:T + NIP].unsqueeze(1).to_broadcast([TT, NP, NIP]), ACT.Copy)\
                                .then_inc(S["gram_done"], 1)
                        elif kind == "ipT":
                            a_(ipTs[:, :], take(name)[0:H * NIP, 0:128], ACT.Copy).then_inc(S["ipT_done"], 1)
                        elif kind == "oT1":
                            a_(o1T[:, :], take(name)[:, 0:256], ACT.Copy).then_inc(S["o1T_done"], 1)

                    def pt_out(n):
                        place = PLACE[n]
                        act.wait_ge(S["pt_done"], place + 1)
                        if place >= 2:
                            act.wait_ge(S["pv_done"], place - 1)
                        J = K0[n // U0] if n < NL0 else TT
                        a_(PTs[0:J, place % 2, :], PT[0:J, :], ACT.Copy).then_inc(S["pts_done"], 1)

                    def exp(n):
                        act.wait_ge(S["sub_done"], PLACE[n] + 1)
                        J, scale = (K0[n // U0], SCALE0) if n < NL0 else (TT, SCALE1)
                        e = SE[:, PLACE[n] % 3, 0:4 * J]
                        a_(e, e, ACT.Exp, scale=scale).then_inc(S["exp_done"], 1)

                    def context_squares(h):
                        act.wait_ge(S["c_in"], 32 * (h + 1))
                        if h:
                            act.wait_ge(S["c_dve"], HB * h)
                        for b in range(HB):
                            if b + h:
                                act.wait_ge(S["c_sq"], HB * h + b)
                            a_(csq, cin[:, b, :], ACT.Square, accum_out=cst[:, 0, b:b + 1]).then_inc(S["c_sq"], 1)

                    for s in range(FIRST, LAST):
                        if unit_at(s - 1) is not None:
                            pt_out(unit_at(s - 1))
                        for name in mid_jobs(s):
                            job(name)
                        if unit_at(s) is not None:
                            exp(unit_at(s))
                        for b in range(GB):
                            if has_l1 and s == tail_slot[b] + 3:
                                act.wait_ge(S["sip_done"], b + 1)
                                e = sip[:, b % 2, :, :]
                                a_(e, e, ACT.Exp).then_inc(S["sipe_done"], 1)
                        for h in preps_at(s):
                            context_squares(h)
                        for name in late_jobs(s):
                            job(name)

                @block.vector
                def _(dve):
                    v = nc.vector
                    chain = [0]

                    def then(ins):
                        chain[0] += 1
                        ins.then_inc(S["d_chain"], 1)
                        dve.wait_ge(S["d_chain"], chain[0])

                    def take(name):
                        dve.wait_ge(S["job_full"], JOB[name] + 1)
                        return bank(name)

                    def norm_stats(k, h):
                        if k == 0:
                            dve.wait_ge(S[f"x_in{h}"], 16)
                        elif (k, h) != (2, 1):
                            dve.wait_ge(S["x_done"], U0 * (k - 1) + NP * (h + 1))
                        x = xres[:, HB * h:HB * h + HB, :]
                        for b in range(HB):
                            last = v.bn_stats(st6[:, b, :], x[:, b, :])
                        then(last)
                        for b in range(HB):
                            last = v.bn_aggr(mv[:, b, :], st6[:, b, :])
                        last.then_inc(S["ln_stats"], 1)
                        dve.wait_ge(S["ln_stats"], REAL_NORMS.index((k, h)) + 1)
                        for b in range(HB):
                            last = v.scalar_tensor_tensor(lt[:, b, :], x[:, b, :], mv[:, b, 0:1], ln_g[:, k, :],
                                                          ALU.subtract, ALU.mult)
                        last.then_inc(S["ln_t"], 1)

                    def norm_out(k, h):
                        i = REAL_NORMS.index((k, h)) + 1
                        dve.wait_ge(S["ln_t"], i)
                        dve.wait_ge(S["rstd_done"], i)
                        rest = lambda ap: ap[:, 128:C].unsqueeze(1).to_broadcast([128, 4, M])
                        for b in range(HB):
                            v.scalar_tensor_tensor(nx[:, b, 0:128], lt[:, b, 0:128], rstd[:, b:b + 1], ln_b[:, k, 0:128],
                                                   ALU.mult, ALU.add)
                            last = v.scalar_tensor_tensor(nx[:, b, 128:256].rearrange("p (r m) -> p r m", m=M),
                                                          rest(lt[:, b, :]), rstd[:, b:b + 1], rest(ln_b[:, k, :]),
                                                          ALU.mult, ALU.add)
                        last.then_inc(S["nx_done"], 1)

                    def l1_input(h):
                        dve.wait_ge(S["down_added"], nth(("down", F * h + F - 1)))
                        x = x1[:, HB * h:HB * h + HB, :]
                        v.tensor_copy(nx[:, :, 0:128], x[:, :, 0:128])
                        for b in range(HB):
                            last = v.tensor_copy(nx[:, b, 128:256].rearrange("p (r m) -> p r m", m=M),
                                                 x[:, b, 128:C].unsqueeze(1).to_broadcast([128, 4, M]))
                        last.then_inc(S["nx_done"], 1)

                    def context_scale(h):
                        dve.wait_ge(S["c_pow"], h + 1)
                        then(v.tensor_scalar(cst[:, 2, :], cst[:, 1, :], EPS_L2, None, ALU.max))
                        then(v.reciprocal(cst[:, 3, :], cst[:, 2, :]))
                        then(v.tensor_scalar(cst[:, 2, :], cst[:, 3, :], is_ip[:, 0:1], not_ip[:, 0:1], ALU.mult, ALU.add))
                        for b in range(HB):
                            v.tensor_scalar(cin[:, b, :], cin[:, b, :], cst[:, 2, b:b + 1], None, ALU.mult)\
                                .then_inc(S["c_dve"], 1)

                    def job(name):
                        kind, i = name[0], name[-1]
                        if kind == "cT":
                            ps = take(name)
                            dve.wait_ge(S["cT_act"], i + 1)
                            w = HB * TS
                            ps = ps[:, 0:2 * w].rearrange("p (c n) -> p c n", c=2)
                            v.tensor_tensor(cT[:, :, 1, w * i:w * i + w], ps, cT[:, :, 0, w * i:w * i + w].bitcast(fp32),
                                            ALU.subtract)
                            for c in range(2):
                                last = v.tensor_copy(cipT[:, c, HB * NIP * i:HB * NIP * (i + 1)].rearrange("p (b n) -> p b n", n=NIP),
                                                     ps[:, c, :].rearrange("p (b t) -> p b t", t=TS)[:, :, TT:T])
                            last.then_inc(S["cT_dve"], 1)
                        elif kind == "xT":
                            ps = take(name)
                            dve.wait_ge(S["nT_act"], NORMS.index(name[1:]) + 1)
                            v.tensor_tensor(nT[:, i, 2, :], ps[:, 0:HT], nT[:, i, 0, :].bitcast(fp32), ALU.subtract)
                            v.tensor_tensor(nT[64:128, i, 1, :], ps[64:128, HT:2 * HT], nT[64:128, i, 1, :].bitcast(fp32),
                                            ALU.subtract).then_inc(S["nT_dve"], 1)
                        elif kind == "v":
                            ps, J = take(name), K0[2 * i // U0]
                            v.tensor_copy(v_sb[0:J, i % 2, :, :, 0:DH],
                                          ps[0:J, :].rearrange("p (b h d) -> p b h d", b=HB, h=4)).then_inc(S["v_done"], 1)
                        elif kind == "ff":
                            h, t = i // F, i % F
                            ps = take(name)
                            dve.wait_ge(S["gelu_done"], nth(name))
                            v.scalar_tensor_tensor(hT[:, nth(name) % 2, :], ps[:, HT:2 * HT], b_1[:, t:t + 1], gl[:, nth(name) % 2, :],
                                                   ALU.add, ALU.mult).then_inc(S["h_done"], 1)
                        elif kind == "down":
                            h, t = i // F, i % F
                            ps = take(name)
                            if t == 0:
                                dve.wait_ge(S["bias_added"], NORMS.index((2, h)) + 1)
                                if has_l1 and h == 0:
                                    dve.wait_ge(S["out_done0"], 16 * HB)
                            else:
                                dve.wait_ge(S["down_added"], nth(name) - 1)
                            x = (x1 if t else xres)[:, HB * h:HB * h + HB, :]
                            v.tensor_tensor(x1[:, HB * h:HB * h + HB, :], ps[:, 0:HB * C].rearrange("p (b c) -> p b c", c=C),
                                            x, ALU.add).then_inc(S["down_added"], 1)
                        elif kind == "k1":
                            ps, r, kw = take(name), name[1], HB * TS
                            r0 = 96 * r
                            own = head_of_row[r0:128, :].unsqueeze(2)
                            for b in range(HB):
                                text = ps[r0:128, TS * b:TS * b + TT].unsqueeze(1)
                                image = ps[r0:128, kw + NIP * b:kw + NIP * b + NIP].unsqueeze(1)
                                v.tensor_tensor(kbd[r0:128, r, b, :, 0:TT], text.to_broadcast([128 - r0, 4, TT]),
                                                own.to_broadcast([128 - r0, 4, TT]), ALU.mult)
                                last = v.tensor_tensor(kbd[r0:128, r, b, :, TT:T],
                                                       image.to_broadcast([128 - r0, 4, NIP]),
                                                       own.to_broadcast([128 - r0, 4, NIP]), ALU.mult)
                            last.then_inc(S["kbd_done"], 1)
                        elif kind == "vip":
                            v.tensor_copy(vip_sb[:, :], take(name)[0:GB * NIP, 0:C]).then_inc(S["vip_done"], 1)
                        elif kind == "ctx1":
                            ps = take(name)
                            dve.wait_ge(S["gram_done"], nth(name))
                            wait_gv_used(dve, i)
                            for h in range(2):
                                v.tensor_copy(gv[:, i % 2, :, (D1 + GS) * h:(D1 + GS) * h + D1],
                                              ps[0:TT, TS:TS + C].rearrange("p (q h d) -> p q h d", h=2, d=D1)[:, :, h, :])
                            v.tensor_tensor(vbd_sb[:, i % 2, :, :],
                                            ps[0:H * NIP, TS + C:TS + 2 * C].rearrange("p (h d) -> p h d", d=D1),
                                            own_head, ALU.mult).then_inc(S["gv_done"], 1)
                        elif kind == "ip":
                            o = o1[:, i % 2, :, :].rearrange("p h d -> p (h d)")
                            v.tensor_tensor(o, take(name)[:, 0:C], o, ALU.add).then_inc(S["o1_done"], 1)
                        elif kind == "y":
                            if i == HB:
                                dve.wait_ge(S["bias_added"], NORMS.index((3, 1)) + 1)
                            v.tensor_tensor(x1[:, i, :], take(name)[:, 0:C], x1[:, i, :], ALU.add).then_inc(S["y_done"], 1)

                    def softmax_in(n):
                        place = PLACE[n]
                        dve.wait_ge(S["s_done"], place + 1)
                        J, step = (K0[n // U0],) * 2 if n < NL0 else (TT, T)
                        e = SE[:, place % 3, 0:4 * J]
                        sc = PS[place % 2][:, 0:4 * step].rearrange("p (i j) -> p i j", j=step)
                        v.tensor_reduce(mx[:, place % 2, :], sc[:, :, 0:J], AX, ALU.max).then_inc(S["mx_done"], 1)
                        dve.wait_ge(S["mx_done"], place + 1)
                        if place >= 3:
                            dve.wait_ge(S["pt_done"], place - 2)
                        last = v.tensor_tensor(e.rearrange("p (i j) -> p i j", j=J), sc[:, :, 0:J],
                                               mx[:, place % 2, :].unsqueeze(2).to_broadcast([128, 4, J]), ALU.subtract)
                        if n >= NL0:
                            b, w = (n - NL0) // W1, (n - NL0) % W1
                            last = v.tensor_copy(sip[:, b % 2, 4 * w:4 * w + 4, :], sc[:, :, TT:T])
                        last.then_inc(S["sub_done"], 1)

                    def unit_out(n):
                        place = PLACE[n]
                        PV = PVS[place % 2]
                        dve.wait_ge(S["pv_done"], place + 1)
                        if n < NL0:
                            o = PV[:, 0:4 * (DH + 1)].rearrange("p (i d) -> p i d", d=DH + 1)
                            v.reciprocal(rs[:, n % 2, :].unsqueeze(2), o[:, :, DH:DH + 1]).then_inc(S["rs_done"], 1)
                            dve.wait_ge(S["rs_done"], place + 1)
                            if n >= 2:
                                dve.wait_ge(S["job_full"], JOB[("ot", n - 2)] + 1)
                            v.tensor_tensor(ON[:, n % 2, :].rearrange("p (i d) -> p i d", d=DH), o[:, :, 0:DH],
                                            rs[:, n % 2, :].unsqueeze(2).to_broadcast([128, 4, DH]), ALU.mult)\
                                .then_inc(S["on_done"], 1)
                            return
                        b, w = (n - NL0) // W1, (n - NL0) % W1
                        o = PV[:, 0:4 * GV].rearrange("p (i d) -> p i d", d=GV)
                        r = rr[:, b % 2, 4 * w:4 * w + 4]
                        v.reciprocal(r.unsqueeze(2), o[:, :, D1 + T:D1 + T + 1]).then_inc(S["rs_done"], 1)
                        dve.wait_ge(S["rs_done"], place + 1)
                        for h in range(2):
                            pv = PV[:, 0:4 * GV].rearrange("p (q d) -> p q d", d=2 * GV)\
                                [:, :, (2 * GV - D1) * h:(2 * GV - D1) * h + D1]
                            v.tensor_tensor(o1[:, b % 2, 4 * w + h:4 * w + 3 + h:2, :], pv,
                                            r[:, h:3 + h:2].unsqueeze(2).to_broadcast([128, 2, D1]), ALU.mult)
                        v.tensor_tensor(sem4[:, b % 2, 4 * w:4 * w + 4, :], o[:, :, D1 + TT:D1 + T],
                                        r.unsqueeze(2).to_broadcast([128, 4, NIP]), ALU.mult)
                        gp = SE[:, place % 3, 0:4 * TT].rearrange("p (i j) -> p i j", j=TT)
                        v.tensor_tensor(gp, o[:, :, D1:D1 + TT], gp, ALU.mult).then_inc(S["on_done"], 1)
                        dve.wait_ge(S["on_done"], place + 1)
                        v.tensor_reduce(qq[:, b % 2, 4 * w:4 * w + 4], gp, AX, ALU.add).then_inc(S["qq_done"], 1)

                    def image_scores(b, part):
                        k, e = b % 2, sip[:, b % 2, :, :]
                        if part == 0:
                            dve.wait_ge(S["n20_done"], b + 1)
                            then(v.tensor_tensor(r20[:, 1, :], r20[:, 0, :], rr[:, k, :], ALU.mult))
                            then(v.tensor_scalar(r20[:, 2, :], r20[:, 1, :], EPS_L2, None, ALU.max))
                            v.reciprocal(r20[:, 3, :], r20[:, 2, :]).then_inc(S["tail_part"], 1)
                        elif part == 1:
                            dve.wait_ge(S["tail_part"], 4 * b + 1)
                            then(v.scalar_tensor_tensor(sem4[:, k, :, :], sem4[:, k, :, :], SEM_SCALE,
                                                        r20[:, 3, :].unsqueeze(2).to_broadcast([128, H, NIP]), ALU.mult, ALU.mult))
                            v.scalar_tensor_tensor(e, e, SCALE1, sem4[:, k, :, :], ALU.mult, ALU.add)\
                                .then_inc(S["tail_part"], 1)
                        else:
                            dve.wait_ge(S["tail_part"], 4 * b + 2)
                            v.tensor_reduce(r20[:, 1, :], e, AX, ALU.max).then_inc(S["tail_part"], 1)
                            dve.wait_ge(S["tail_part"], 4 * b + 3)
                            v.tensor_tensor(e, e, r20[:, 1, :].unsqueeze(2).to_broadcast([128, H, NIP]), ALU.subtract)\
                                .then_inc(S["sip_done"], 1)

                    def image_probs(b, part):
                        e = sip[:, b % 2, :, :]
                        if part == 0:
                            dve.wait_ge(S["sipe_done"], b + 1)
                            then(v.tensor_reduce(r20[:, 2, :], e, AX, ALU.add))
                            v.reciprocal(r20[:, 3, :], r20[:, 2, :]).then_inc(S["tail_part"], 1)
                        else:
                            dve.wait_ge(S["tail_part"], 4 * b + 4)
                            then(v.tensor_scalar(r20[:, 2, :], r20[:, 3, :], fside[:, 0:1], None, ALU.mult))
                            v.tensor_tensor(e, e, r20[:, 2, :].unsqueeze(2).to_broadcast([128, H, NIP]), ALU.mult)\
                                .then_inc(S["mask_done"], 1)

                    for s in range(FIRST, LAST):
                        if unit_at(s - 3) is not None:
                            unit_out(unit_at(s - 3))
                        if unit_at(s) is not None:
                            softmax_in(unit_at(s))
                        for name in mid_jobs(s):
                            job(name)
                        for h in preps_at(s):
                            context_scale(h)
                        for name in late_jobs(s):
                            job(name)
                        for k, h in norms_at(s):
                            if k == 3:
                                l1_input(h)
                        for k, h in norms_at(s - 1):
                            if k < 3:
                                norm_out(k, h)
                        for k, h in norms_at(s):
                            if k < 3:
                                norm_stats(k, h)
                        for b in range(GB):
                            part = s - tail_slot[b]
                            if has_l1 and 0 <= part < 3:
                                image_scores(b, part)
                            if has_l1 and 3 <= part < 5:
                                image_probs(b, part - 3)

                @block.gpsimd
                def _(pool):
                    g = nc.gpsimd
                    own = [0]

                    def then(ins):
                        own[0] += 1
                        ins.then_inc(S["pool_own"], 1)
                        pool.wait_ge(S["pool_own"], own[0])

                    def rstd_of(k, h):
                        pool.wait_ge(S["ln_stats"], REAL_NORMS.index((k, h)) + 1)
                        then(g.tensor_scalar(vp[:, :].unsqueeze(2), mv[:, :, 1:2], EPS_LN, None, ALU.add))
                        g.tensor_tensor(rstd[:, :], vp[:, :], p_mhalf[:, 0:HB], ALU.pow).then_inc(S["rstd_done"], 1)

                    def add_bias(k, h):
                        x = xres[:, HB * h:HB * h + HB, :]
                        if k < 3:
                            pool.wait_ge(S["ln_t"], REAL_NORMS.index((k, h)) + 1)
                        else:
                            x = x1[:, HB * h:HB * h + HB, :]
                            pool.wait_ge(S["nx_done"], NORMS.index((k, h)) + 1)
                        g.tensor_tensor(x, x, bias[:, k, :].unsqueeze(1).to_broadcast([128, HB, C]), ALU.add)\
                            .then_inc(S["bias_added"], 1)

                    def add_out(n):
                        a, h = n // U0, n // NP % 2
                        pool.wait_ge(S["wos_done"], n + 1)
                        if n % NP == 0 and n > 0:
                            pool.wait_ge(S["bias_added"], NORMS.index((a, h)) + 1)
                        if n >= 1:
                            pool.wait_ge(S["x_done"], n)
                        x = xres[:, HB * h:HB * h + HB, :]
                        g.tensor_tensor(x, x, WOs[:, n % 2, :, :], ALU.add).then_inc(S["x_done"], 1)

                    for s in range(FIRST, LAST):
                        for k, h in norms_at(s - 1):
                            if k < 3:
                                rstd_of(k, h)
                                add_bias(k, h)
                        for k, h in norms_at(s):
                            if k == 3:
                                add_bias(k, h)
                        for h in preps_at(s):
                            pool.wait_ge(S["c_sq"], HB * (h + 1))
                            g.tensor_tensor(cst[:, 1, :], cst[:, 0, :], p_half[0:TS, 0:HB], ALU.pow).then_inc(S["c_pow"], 1)
                        if l0_unit(s - 5) is not None:
                            add_out(l0_unit(s - 5))
                        for b in range(GB):
                            if has_l1 and s == tail_slot[b] - 1:
                                pool.wait_ge(S["qq_done"], W1 * (b + 1))
                                g.tensor_tensor(r20[:, 0, :], qq[:, b % 2, :], p_half[:, :], ALU.pow).then_inc(S["n20_done"], 1)

            nc.sync.sem_clear(range(nums[0], nums[-1] + 1))
            nc.all_engine_barrier()

        groups = lambda t: t.rearrange("(g b) n c -> g b n c", b=GB)
        group_step(False, False, True, None, None, x_dram[0:GB], None)
        group_step(True, False, True, x_dram[0:GB], ctx_dram[0:GB], x_dram[GB:2 * GB], None)
        with nc.Fori(0, GROUPS - 2) as grp:
            group_step(True, True, True, groups(x_dram[GB:B])[grp], groups(ctx_dram[GB:B])[grp],
                       groups(x_dram[2 * GB:B])[grp], groups(out)[grp])
        group_step(True, True, False, x_dram[B - GB:B], ctx_dram[B - GB:B], None, out[B - 2 * GB:B - GB])
        group_step(False, True, False, None, None, None, out[B - GB:B])


_INS = ['x', 'ctx_2048', 'fside_S_0',
        'L0_xattn_a1_wq', 'L0_xattn_a1_wk', 'L0_xattn_a1_wv', 'L0_xattn_a1_wo', 'L0_xattn_a1_bo',
        'L0_xattn_a2_wq', 'L0_xattn_a2_wk', 'L0_xattn_a2_wv', 'L0_xattn_a2_wo', 'L0_xattn_a2_bo',
        'L0_xattn_ff_w1', 'L0_xattn_ff_b1', 'L0_xattn_ff_w2', 'L0_xattn_ff_b2',
        'L0_xattn_ln1_g', 'L0_xattn_ln1_b', 'L0_xattn_ln2_g', 'L0_xattn_ln2_b', 'L0_xattn_ln3_g', 'L0_xattn_ln3_b',
        'L1_xattn_W_q', 'L1_xattn_W_k', 'L1_xattn_W_v', 'L1_xattn_W_k_ip', 'L1_xattn_W_v_ip', 'L1_xattn_W_out',
        'L1_xattn_b_out']


def kernel(**inputs):
    import numpy as _np
    import concourse.bacc as _bacc
    from concourse import mybir as _mybir
    from concourse.bass_utils import run_bass_kernel_spmd as _run

    nc = _bacc.Bacc("TRN2", target_bir_lowering=False, num_devices=1, dynamic_dma_scratch_size=1024)
    arrays, aps = {}, {}
    for name in _INS:
        a = _np.ascontiguousarray(inputs[name])
        arrays[f"in_{name}_dram"] = a
        aps[name] = nc.dram_tensor(f"in_{name}_dram", a.shape, _mybir.dt.from_np(a.dtype), kind="ExternalInput").ap()
    out = nc.dram_tensor("out_dram", inputs["x"].shape, _mybir.dt.float32, kind="ExternalOutput").ap()
    xattn_program(nc, aps, out)
    r = _run(nc, [arrays], core_ids=[0])
    return r.results[0]["out_dram"]
```
